# Optimizing a Trainium2 kernel written in Bass

```python
import numpy as np
import jax
import jax.numpy as jnp

def _softmax(x, axis=-1):
    return jax.nn.softmax(x, axis=axis)

def _gelu(x):
    return jax.nn.gelu(x, approximate=True)

def _silu(x):
    return jax.nn.silu(x)

def _sigmoid(x):
    return jax.nn.sigmoid(x)

def _layernorm(x, axis=-1, eps=1e-05):
    m = jnp.mean(x, axis=axis, keepdims=True)
    v = jnp.var(x, axis=axis, keepdims=True)
    return (x - m) / jnp.sqrt(v + eps)

def _scatter_add(tgt, idx, src, axis=0):
    return tgt.at[idx].add(src)

def _segment_sum(src, seg, n):
    return jax.ops.segment_sum(src, seg, n)
kernel_name = 'mk_pixart_seq_d2_seqx_r8_760e96'

def setup_inputs(seed: int=0):
    np.random.seed(seed)
    _w = jnp.asarray

    def _rec_inputs():
        import jax
        import jax.numpy as jnp
        _rk = jax.random.key(seed)
        x = -0.0002928 + 1 * jax.random.normal(jax.random.fold_in(_rk, 1), (64, 128, 128), jnp.float32)
        _lenS = 128 - jax.random.randint(jax.random.fold_in(_rk, 7), (64,), 0, max(1, 128 // 4) + 1, jnp.int32)
        _lenS2 = 77 - jax.random.randint(jax.random.fold_in(_rk, 8), (64,), 0, max(1, 77 // 4) + 1, jnp.int32)
        cond_1024 = 0.000887014 + 1.03683 * jax.random.normal(jax.random.fold_in(_rk, 11), (64, 128), jnp.float32)
        _ctx_1024P = jax.random.normal(jax.random.fold_in(_rk, 12), (64, 16, 128), jnp.float32)
        _ctx_1024c = jax.random.dirichlet(jax.random.fold_in(_rk, 512), 0.3 * jnp.ones((16,), jnp.float32), (64, 77))
        _ctx_1024t = jnp.einsum('bsk,bkd->bsd', _ctx_1024c, _ctx_1024P)
        _ctx_1024t = _ctx_1024t * jax.lax.rsqrt(jnp.mean(jnp.square(_ctx_1024t)) + 1e-12) * 0.953939
        ctx_1024 = -0.00606593 + 0.997213 * (_ctx_1024t + 0.3 * jax.random.normal(jax.random.fold_in(_rk, 612), (64, 77, 128), jnp.float32))
        _validS = jnp.arange(128)[None, :] < _lenS[:, None]
        _validS2 = jnp.arange(77)[None, :] < _lenS2[:, None]
        _causal = jnp.tril(jnp.ones((128, 128), dtype=bool))
        mask_BxS2_bf1 = jnp.ones((64, 77), dtype=bool)
        mask_SxS_bk0 = jnp.logical_not(jnp.broadcast_to(_validS[0:1, :], (128, 128)))
        return (x, cond_1024, ctx_1024, mask_BxS2_bf1, mask_SxS_bk0)
    x, cond_1024, ctx_1024, mask_BxS2_bf1, mask_SxS_bk0 = _rec_inputs()

    def _L0_xcond_setup():
        import jax, jax.numpy as jnp
        import numpy as np
        B, N, D, H, LC = (2, 128, 128, 16, 77)
        HD = D // H
        BLOCK = 16
        ROPE_BASE = 10000.0
        EPS = 1e-05

        def _block_diff_mask(n, block_size):
            idx = np.arange(2 * n)
            q = idx[:, None]
            kv = idx[None, :]
            fq = q >= n
            fkv = kv >= n
            bq = np.where(fq, (q - n) // block_size, q // block_size)
            bkv = np.where(fkv, (kv - n) // block_size, kv // block_size)
            block_diagonal = (bq == bkv) & (fq == fkv)
            offset_block_causal = (bq > bkv) & fkv & ~fq
            block_causal = (bq >= bkv) & fq & fkv
            return jnp.asarray(block_diagonal | offset_block_causal | block_causal)

        def _rope_tables(n):
            inv_freq = 1.0 / ROPE_BASE ** (np.arange(0, HD, 2, dtype=np.float32) / HD)
            freqs = np.outer(np.arange(n, dtype=np.float32), inv_freq)
            emb = np.concatenate([freqs, freqs], axis=-1)
            cos = jnp.asarray(np.cos(emb), jnp.float32)[None, :, None, :]
            sin = jnp.asarray(np.sin(emb), jnp.float32)[None, :, None, :]
            return (cos, sin)

        def _ln(x, w):
            xf = x.astype(jnp.float32)
            mu = jnp.mean(xf, axis=-1, keepdims=True)
            var = jnp.mean(jnp.square(xf - mu), axis=-1, keepdims=True)
            y = (xf - mu) * jax.lax.rsqrt(var + EPS)
            return y * w[None, None, :]

        def _apply_rope(t, cos, sin):
            t1, t2 = jnp.split(t, 2, axis=-1)
            rot = jnp.concatenate([-t2, t1], axis=-1)
            return t * cos + rot * sin

        def _attn(q, k, v, mask):
            scale = 1.0 / np.sqrt(HD)
            s = jnp.einsum('bqhd,bkhd->bhqk', q, k) * scale
            s = jnp.where(mask, s, jnp.finfo(s.dtype).min)
            a = jax.nn.softmax(s, axis=-1)
            return jnp.einsum('bhqk,bkhd->bqhd', a, v)
        key = jax.random.key(seed)
        ks = jax.random.split(key, 16)
        w = lambda k, shp: jax.random.normal(k, shp, jnp.float32) * 0.02
        inp = {'x': jax.random.normal(ks[0], (B, 2 * N, D), jnp.float32), 'cond_global': jax.random.normal(ks[1], (B, D), jnp.float32), 'cond_tokens': jax.random.normal(ks[2], (B, LC, D), jnp.float32), 'adaLN_W': w(ks[3], (D, 9 * D)), 'adaLN_b': w(ks[4], (9 * D,)), 'norm1_w': jnp.ones((D,), jnp.float32), 'qkv_W': w(ks[5], (D, 3 * D)), 'attn_out_W': w(ks[6], (D, D)), 'normc_w': jnp.ones((D,), jnp.float32), 'cq_W': w(ks[7], (D, D)), 'ck_W': w(ks[8], (D, D)), 'cv_W': w(ks[9], (D, D)), 'co_W': w(ks[10], (D, D)), 'norm2_w': jnp.ones((D,), jnp.float32), 'mlp_W1': w(ks[11], (D, 4 * D)), 'mlp_b1': w(ks[12], (4 * D,)), 'mlp_W2': w(ks[13], (4 * D, D)), 'mlp_b2': w(ks[14], (D,)), 'cond_kv_mask': jnp.ones((B, LC), bool), 'attn_mask': _block_diff_mask(N, BLOCK)}
        return inp
    _L0_xcond_all = _L0_xcond_setup()
    _L0_xcond_in = {k: v for k, v in _L0_xcond_all.items() if k in ('adaLN_W', 'adaLN_b', 'norm1_w', 'qkv_W', 'attn_out_W', 'normc_w', 'cq_W', 'ck_W', 'cv_W', 'co_W', 'norm2_w', 'mlp_W1', 'mlp_b1', 'mlp_W2', 'mlp_b2')}
    del _L0_xcond_all

    def _L1_xcond_setup():
        import jax, jax.numpy as jnp
        import numpy as np
        EPS = 1e-05

        def _ada_ln(x, c, W_ss, b_ss):
            mu = jnp.mean(x, axis=-1, keepdims=True)
            var = jnp.mean((x - mu) ** 2, axis=-1, keepdims=True)
            h = (x - mu) / jnp.sqrt(var + EPS)
            ss = jax.nn.silu(c) @ W_ss + b_ss
            scale, bias = jnp.split(ss, 2, axis=-1)
            return (1.0 + scale)[:, None, :] * h + bias[:, None, :]
        key = jax.random.key(seed)
        ks = jax.random.split(key, 12)
        B, Lq, Lkv, H = (8, 256, 64, 128)
        s = 0.02
        return {'x_q': jax.random.normal(ks[0], (B, Lq, H), jnp.float32), 'x_kv': jax.random.normal(ks[1], (B, Lkv, H), jnp.float32), 't_vec': jax.random.normal(ks[2], (B, H), jnp.float32), 'Wq': jax.random.normal(ks[3], (H, H), jnp.float32) * s, 'bq': jnp.zeros((H,), jnp.float32), 'Wkv': jax.random.normal(ks[4], (H, 2 * H), jnp.float32) * s, 'bkv': jnp.zeros((2 * H,), jnp.float32), 'Wp': jax.random.normal(ks[5], (H, H), jnp.float32) * s, 'bp': jnp.zeros((H,), jnp.float32), 'Wss_q': jax.random.normal(ks[6], (H, 2 * H), jnp.float32) * s, 'bss_q': jnp.zeros((2 * H,), jnp.float32), 'Wss_kv': jax.random.normal(ks[7], (H, 2 * H), jnp.float32) * s, 'bss_kv': jnp.zeros((2 * H,), jnp.float32)}
    _L1_xcond_all = _L1_xcond_setup()
    _L1_xcond_in = {k: v for k, v in _L1_xcond_all.items() if k in ('Wq', 'bq', 'Wkv', 'bkv', 'Wp', 'bp', 'Wss_q', 'bss_q', 'Wss_kv', 'bss_kv')}
    del _L1_xcond_all
    return {'x': x, 'cond_1024': cond_1024, 'ctx_1024': ctx_1024, 'mask_BxS2_bf1': mask_BxS2_bf1, 'mask_SxS_bk0': mask_SxS_bk0, 'L0_xcond_adaLN_W': _L0_xcond_in['adaLN_W'], 'L0_xcond_adaLN_b': _L0_xcond_in['adaLN_b'], 'L0_xcond_norm1_w': _L0_xcond_in['norm1_w'], 'L0_xcond_qkv_W': _L0_xcond_in['qkv_W'], 'L0_xcond_attn_out_W': _L0_xcond_in['attn_out_W'], 'L0_xcond_normc_w': _L0_xcond_in['normc_w'], 'L0_xcond_cq_W': _L0_xcond_in['cq_W'], 'L0_xcond_ck_W': _L0_xcond_in['ck_W'], 'L0_xcond_cv_W': _L0_xcond_in['cv_W'], 'L0_xcond_co_W': _L0_xcond_in['co_W'], 'L0_xcond_norm2_w': _L0_xcond_in['norm2_w'], 'L0_xcond_mlp_W1': _L0_xcond_in['mlp_W1'], 'L0_xcond_mlp_b1': _L0_xcond_in['mlp_b1'], 'L0_xcond_mlp_W2': _L0_xcond_in['mlp_W2'], 'L0_xcond_mlp_b2': _L0_xcond_in['mlp_b2'], 'L1_xcond_Wq': _L1_xcond_in['Wq'], 'L1_xcond_bq': _L1_xcond_in['bq'], 'L1_xcond_Wkv': _L1_xcond_in['Wkv'], 'L1_xcond_bkv': _L1_xcond_in['bkv'], 'L1_xcond_Wp': _L1_xcond_in['Wp'], 'L1_xcond_bp': _L1_xcond_in['bp'], 'L1_xcond_Wss_q': _L1_xcond_in['Wss_q'], 'L1_xcond_bss_q': _L1_xcond_in['bss_q'], 'L1_xcond_Wss_kv': _L1_xcond_in['Wss_kv'], 'L1_xcond_bss_kv': _L1_xcond_in['bss_kv']}

def reference(x, cond_1024, ctx_1024, mask_BxS2_bf1, mask_SxS_bk0, L0_xcond_adaLN_W, L0_xcond_adaLN_b, L0_xcond_norm1_w, L0_xcond_qkv_W, L0_xcond_attn_out_W, L0_xcond_normc_w, L0_xcond_cq_W, L0_xcond_ck_W, L0_xcond_cv_W, L0_xcond_co_W, L0_xcond_norm2_w, L0_xcond_mlp_W1, L0_xcond_mlp_b1, L0_xcond_mlp_W2, L0_xcond_mlp_b2, L1_xcond_Wq, L1_xcond_bq, L1_xcond_Wkv, L1_xcond_bkv, L1_xcond_Wp, L1_xcond_bp, L1_xcond_Wss_q, L1_xcond_bss_q, L1_xcond_Wss_kv, L1_xcond_bss_kv):
    import jax
    import jax.numpy as jnp

    def _L0_xcond_ref(x, cond_global, cond_tokens, adaLN_W, adaLN_b, norm1_w, qkv_W, attn_out_W, normc_w, cq_W, ck_W, cv_W, co_W, norm2_w, mlp_W1, mlp_b1, mlp_W2, mlp_b2, cond_kv_mask, attn_mask):
        import jax, jax.numpy as jnp
        import numpy as np
        B, N, D, H, LC = (2, 128, 128, 16, 77)
        HD = D // H
        BLOCK = 16
        ROPE_BASE = 10000.0
        EPS = 1e-05

        def _block_diff_mask(n, block_size):
            idx = np.arange(2 * n)
            q = idx[:, None]
            kv = idx[None, :]
            fq = q >= n
            fkv = kv >= n
            bq = np.where(fq, (q - n) // block_size, q // block_size)
            bkv = np.where(fkv, (kv - n) // block_size, kv // block_size)
            block_diagonal = (bq == bkv) & (fq == fkv)
            offset_block_causal = (bq > bkv) & fkv & ~fq
            block_causal = (bq >= bkv) & fq & fkv
            return jnp.asarray(block_diagonal | offset_block_causal | block_causal)

        def _rope_tables(n):
            inv_freq = 1.0 / ROPE_BASE ** (np.arange(0, HD, 2, dtype=np.float32) / HD)
            freqs = np.outer(np.arange(n, dtype=np.float32), inv_freq)
            emb = np.concatenate([freqs, freqs], axis=-1)
            cos = jnp.asarray(np.cos(emb), jnp.float32)[None, :, None, :]
            sin = jnp.asarray(np.sin(emb), jnp.float32)[None, :, None, :]
            return (cos, sin)

        def _ln(x, w):
            xf = x.astype(jnp.float32)
            mu = jnp.mean(xf, axis=-1, keepdims=True)
            var = jnp.mean(jnp.square(xf - mu), axis=-1, keepdims=True)
            y = (xf - mu) * jax.lax.rsqrt(var + EPS)
            return y * w[None, None, :]

        def _apply_rope(t, cos, sin):
            t1, t2 = jnp.split(t, 2, axis=-1)
            rot = jnp.concatenate([-t2, t1], axis=-1)
            return t * cos + rot * sin

        def _attn(q, k, v, mask):
            scale = 1.0 / np.sqrt(HD)
            s = jnp.einsum('bqhd,bkhd->bhqk', q, k) * scale
            s = jnp.where(mask, s, jnp.finfo(s.dtype).min)
            a = jax.nn.softmax(s, axis=-1)
            return jnp.einsum('bhqk,bkhd->bqhd', a, v)
        b, s, d = x.shape
        n = s // 2
        mod = (cond_global @ adaLN_W + adaLN_b)[:, None, :]
        sh_msa, sc_msa, g_msa, sh_x, sc_x, g_x, sh_mlp, sc_mlp, g_mlp = jnp.split(mod, 9, axis=-1)
        x_norm = _ln(x, norm1_w) * (1 + sc_msa) + sh_msa
        cos, sin = _rope_tables(n)

        def qkv(h):
            t = (h @ qkv_W).reshape(b, n, 3, H, HD)
            q, k, v = (t[:, :, 0], t[:, :, 1], t[:, :, 2])
            return (_apply_rope(q, cos, sin), _apply_rope(k, cos, sin), v)
        q1, k1, v1 = qkv(x_norm[:, :n])
        q2, k2, v2 = qkv(x_norm[:, n:])
        q = jnp.concatenate([q1, q2], axis=1)
        k = jnp.concatenate([k1, k2], axis=1)
        v = jnp.concatenate([v1, v2], axis=1)
        self_out = _attn(q, k, v, attn_mask[None, None]).reshape(b, s, d) @ attn_out_W
        x = x + g_msa * self_out
        xc = _ln(x, normc_w) * (1 + sc_x) + sh_x
        qc = (xc @ cq_W).reshape(b, s, H, HD)
        kc = (cond_tokens @ ck_W).reshape(b, LC, H, HD)
        vc = (cond_tokens @ cv_W).reshape(b, LC, H, HD)
        cross = _attn(qc, kc, vc, cond_kv_mask[:, None, None, :]).reshape(b, s, d) @ co_W
        x = x + g_x * cross
        xm = _ln(x, norm2_w) * (1 + sc_mlp) + sh_mlp
        h = jax.nn.gelu(xm @ mlp_W1 + mlp_b1, approximate=True)
        mlp_out = h @ mlp_W2 + mlp_b2
        return x + g_mlp * mlp_out

    def _L1_xcond_ref(x_q, x_kv, t_vec, Wq, bq, Wkv, bkv, Wp, bp, Wss_q, bss_q, Wss_kv, bss_kv):
        import jax, jax.numpy as jnp
        import numpy as np
        EPS = 1e-05

        def _ada_ln(x, c, W_ss, b_ss):
            mu = jnp.mean(x, axis=-1, keepdims=True)
            var = jnp.mean((x - mu) ** 2, axis=-1, keepdims=True)
            h = (x - mu) / jnp.sqrt(var + EPS)
            ss = jax.nn.silu(c) @ W_ss + b_ss
            scale, bias = jnp.split(ss, 2, axis=-1)
            return (1.0 + scale)[:, None, :] * h + bias[:, None, :]
        B, Lq, H = x_q.shape
        Lkv = x_kv.shape[1]
        nh = 16
        dh = H // nh
        xq = _ada_ln(x_q, t_vec, Wss_q, bss_q)
        xkv = _ada_ln(x_kv, t_vec, Wss_kv, bss_kv)
        q = (xq @ Wq + bq).reshape(B, Lq, nh, dh)
        kv = (xkv @ Wkv + bkv).reshape(B, Lkv, 2, nh, dh)
        k = kv[:, :, 0]
        v = kv[:, :, 1]
        scores = jnp.einsum('bqhd,bkhd->bhqk', q, k) / jnp.sqrt(jnp.float32(dh))
        attn = jax.nn.softmax(scores, axis=-1)
        out = jnp.einsum('bhqk,bkhd->bqhd', attn, v).reshape(B, Lq, H)
        return x_q + (out @ Wp + bp)
    x = _L0_xcond_ref(x, cond_1024, ctx_1024, L0_xcond_adaLN_W, L0_xcond_adaLN_b, L0_xcond_norm1_w, L0_xcond_qkv_W, L0_xcond_attn_out_W, L0_xcond_normc_w, L0_xcond_cq_W, L0_xcond_ck_W, L0_xcond_cv_W, L0_xcond_co_W, L0_xcond_norm2_w, L0_xcond_mlp_W1, L0_xcond_mlp_b1, L0_xcond_mlp_W2, L0_xcond_mlp_b2, mask_BxS2_bf1, mask_SxS_bk0)
    x = _L1_xcond_ref(x, ctx_1024, cond_1024, L1_xcond_Wq, L1_xcond_bq, L1_xcond_Wkv, L1_xcond_bkv, L1_xcond_Wp, L1_xcond_bp, L1_xcond_Wss_q, L1_xcond_bss_q, L1_xcond_Wss_kv, L1_xcond_bss_kv)
    return x

_drawn_inputs = setup_inputs


def setup_inputs(seed=0):
    import zlib

    import numpy as np

    out = dict(_drawn_inputs(seed))
    spreads = {'L0_xcond_norm1_w': (1.0, 0.6),
     'L0_xcond_normc_w': (1.0, 0.6),
     'L0_xcond_norm2_w': (1.0, 0.6),
     'L1_xcond_bq': (0.0, 2.0),
     'L1_xcond_bkv': (0.0, 2.0),
     'L1_xcond_bp': (0.0, 2.0),
     'L1_xcond_bss_q': (0.0, 2.0),
     'L1_xcond_bss_kv': (0.0, 2.0)}
    factors = {'cond_1024': 2.852,
     'L0_xcond_adaLN_W': 3.105,
     'L0_xcond_adaLN_b': 8.0,
     'L0_xcond_qkv_W': 6.011,
     'L0_xcond_attn_out_W': 5.996,
     'L0_xcond_cq_W': 8.0,
     'L0_xcond_ck_W': 8.0,
     'L0_xcond_cv_W': 8.0,
     'L0_xcond_co_W': 8.0,
     'L0_xcond_mlp_W1': 4.201,
     'L0_xcond_mlp_b1': 8.0,
     'L0_xcond_mlp_W2': 4.089,
     'L0_xcond_mlp_b2': 27.003,
     'L1_xcond_Wq': 64.0,
     'L1_xcond_Wss_q': 64.0,
     'L1_xcond_Wss_kv': 33.338,
     'L1_xcond_Wkv': 5.159,
     'L1_xcond_Wp': 4.691}
    for name, (base, spread) in spreads.items():
        noise = np.random.default_rng([zlib.crc32(name.encode()), seed]).standard_normal(out[name].shape)
        drawn = base * np.exp(spread * noise) if base else spread * noise
        out[name] = jnp.asarray(drawn.astype(out[name].dtype))
    for name, factor in factors.items():
        out[name] = (out[name] * factor).astype(out[name].dtype)
    return out
```

```python
from contextlib import ExitStack

import numpy as np
import concourse.bass as bass
from concourse import mybir

F32 = mybir.dt.float32
F32R = mybir.dt.float32r
BF16 = mybir.dt.bfloat16
U8 = mybir.dt.uint8
ALU = mybir.AluOpType
ACT = mybir.ActivationFunctionType
AX_X = mybir.AxisListType.X

B, S, D = 64, 128, 128
SC = 77
H, HD = 16, 8
G = 4
NG = B // G
NT, NC = G * S, G * SC
F = 4 * D
EPS = 1e-5
SCALE = 1.0 / float(np.sqrt(HD))
BIG = 2.0 ** 126
HIGH = ((0, 1, 2), (0, 3, 5))
MID = ((3, 4), (1, 4))
LOW = (5, 2)
SLOTS = 8


VEC_ROW = {"L0_xcond_adaLN_b": 0, "L1_xcond_bss_q": 9, "L1_xcond_bss_kv": 11, "L0_xcond_norm1_w": 13,
           "L0_xcond_normc_w": 14, "L0_xcond_norm2_w": 15, "L0_xcond_mlp_b2": 16, "L1_xcond_bq": 17, "L1_xcond_bp": 18,
           "L0_xcond_mlp_b1": 19, "L1_xcond_bkv": 23}
NVEC = 25


def for_groups(eng, body):
    body(0, 0)
    with eng.Fori(0, (NG - 2) // 2) as t:
        body(2 * t + 1, 1)
        body(2 * t + 2, 0)
    body(NG - 1, 1)


class Core:
    pass


def is_first(i):
    return isinstance(i, int) and i == 0


def is_last(i):
    return isinstance(i, int) and i == NG - 1


def wait_past(eng, sem, value, i, behind=0):
    if isinstance(value, int) and value <= 0:
        return
    eng.wait_ge(sem, value)


def setup_phase(nc, c, ins, ctx):
    s = lambda n: ctx.enter_context(nc.semaphore(n))
    loads = s("su_loads")
    zeroed, eyed, ready = s("su_zeroed"), s("su_eyed"), s("su_ready")
    psum_full, cond_t, silu_e, silu_d, copied = (s("su_psum_full"), s("su_cond_t"), s("su_silu_e"),
                                                 s("su_silu_d"), s("su_copied"))
    made, masks, mask_ps = s("su_made"), s("su_masks"), s("su_mask_ps")
    steps = s("su_steps")
    n_loads = [0]
    vec = lambda name, n=0: c.vec[:, c.vec_row[name] + n:c.vec_row[name] + n + 1]
    with nc.Block() as block:
        @block.sync
        def _(sp):
            def load(dst, src):
                sp.dma_start(dst, src).then_inc(loads, 16)
                n_loads[0] += 16
            load(c.cond[:], ins["cond_1024"])
            load(c.ada_w[:], ins["L0_xcond_adaLN_W"])
            load(c.wqkv[:], ins["L0_xcond_qkv_W"])
            for n, name in enumerate(("cq_W", "ck_W", "cv_W")):
                load(c.w0[:, n + 1, :], ins["L0_xcond_" + name])
            load(c.w1[:], ins["L0_xcond_mlp_W1"])
            load(c.w2[:], ins["L0_xcond_mlp_W2"].rearrange("(f p) n -> p f n", p=128))
            load(c.wq[:], ins["L1_xcond_Wq"])
            load(c.wkv[:], ins["L1_xcond_Wkv"])
            load(c.wp_in[:], ins["L1_xcond_Wp"])
            for dst, name in ((c.w0[:, 0, :], "L0_xcond_attn_out_W"), (c.w0[:, 4, :], "L0_xcond_co_W"), (c.wp[:], "L1_xcond_Wp")):
                rows = ins[name].rearrange("(cc g e) n -> cc g e n", cc=2, g=4)
                for g in range(4):
                    for cc in range(2):
                        load(dst[32 * g + 16 * cc:32 * g + 16 * cc + 16, :], rows[cc, g])
            load(c.wss[:, 0, :], ins["L1_xcond_Wss_q"])
            load(c.wss[:, 1, :], ins["L1_xcond_Wss_kv"])
            for name, first in c.vec_row.items():
                n = ins[name].shape[0] // 128
                load(c.vec_rows[first:first + n, :], ins[name].rearrange("(c p) -> c p", p=128))
            load(c.cos[:], ins["cos"])
            load(c.sin[:], ins["sin"])
            load(c.mask8[:].bitcast(mybir.dt.int32), ins["mask_SxS_bk0"])
            load(c.key8[0:B, :], ins["mask_BxS2_bf1"])

        @block.gpsimd
        def _(pool):
            nc.gpsimd.memset(c.eye[:], 0.0).then_inc(zeroed, 1)
            nc.gpsimd.memset(c.pick[:], 0.0).then_inc(zeroed, 1)
            pool.wait_ge(zeroed, 2)
            nc.gpsimd.affine_select(out=c.eye[:], in_=c.eye[:], compare_op=ALU.not_equal, fill=1.0,
                                    base=0, pattern=[[-1, 128]], channel_multiplier=1).then_inc(eyed, 1)
            for n, a in enumerate((0, 1, 2, 4, 5, 6)):
                nc.gpsimd.affine_select(out=c.pick[:], in_=c.pick[:], compare_op=ALU.not_equal,
                                        fill=1.0, base=-16 * a, pattern=[[-1, 16]],
                                        channel_multiplier=1).then_inc(eyed, 1)
                pool.wait_ge(eyed, n + 2)

        @block.vector
        def _(dve):
            v = nc.vector
            v.memset(c.mean[:], 1.0 / D)
            v.memset(c.key_rows[:], 0.0)
            v.memset(c.eps[:], EPS)
            v.memset(c.vz[:], 0.0)
            v.memset(c.parts[:], 0.0)
            v.memset(c.nm[:], 0.0)
            v.memset(c.ones_z[:], 0.0).then_inc(steps, 1)
            dve.wait_ge(steps, 1)
            for hh in range(4):
                v.memset(c.ones_z[:, hh, HD * hh:HD * hh + HD], 1.0)
            dve.wait_ge(eyed, 7)
            v.tensor_scalar(c.centre[:], c.eye[:], -1.0 / D, None, ALU.add)
            v.tensor_copy(c.eye_bf[:], c.eye[:])
            v.tensor_copy(c.head_sel[:], c.pick[:].unsqueeze(2).broadcast_to([128, H, S]))
            dve.wait_ge(loads, n_loads[0])
            v.tensor_scalar(c.mask_nat[:], c.mask8[:], -1.0, BIG, ALU.add, ALU.mult).then_inc(masks, 1)
            v.tensor_scalar(c.key_rows[0:B, :], c.key8[0:B, :], -1.0, BIG, ALU.add, ALU.mult)
            v.tensor_scalar(c.cosq[:], c.cos[:], SCALE, None, ALU.mult)
            v.tensor_scalar(c.sinq[:], c.sin[:], SCALE, None, ALU.mult).then_inc(ready, 1)
            dve.wait_ge(psum_full, 1)
            v.tensor_copy(c.vec[:], c.ps_pj[1][:, 0:NVEC]).then_inc(cond_t, 1)
            v.tensor_copy(c.cond_t[:, 0, :], c.ps_pj[0][:, 0:B]).then_inc(cond_t, 1)
            dve.wait_ge(silu_e, 1)
            v.tensor_scalar(c.cond_t[:, 1, :], c.cond_t[:, 1, :], 1.0, None, ALU.add).then_inc(silu_d, 1)
            dve.wait_ge(silu_d, 1)
            v.reciprocal(c.cond_t[:, 1, :], c.cond_t[:, 1, :]).then_inc(silu_d, 1)
            dve.wait_ge(silu_d, 2)
            v.tensor_tensor(c.cond_t[:, 1, :], c.cond_t[:, 0, :], c.cond_t[:, 1, :], ALU.mult).then_inc(silu_d, 1)
            dve.wait_ge(mask_ps, 1)
            v.tensor_copy(c.mask_t[:], c.ps_mt16[:, 0:S])
            v.tensor_copy(c.key_bias[0:SC, :], c.ps_mt16[0:SC, S:S + B])
            for m in range(13):
                dve.wait_ge(made, m + 1)
                bias = c.vec[:, m:m + 1]
                v.tensor_scalar(c.mod[:, m, :], c.ps_pj[m % 2][:, 0:B], bias, None, ALU.add).then_inc(copied, 1)
            dve.wait_ge(copied, 13)
            for n, m in enumerate((1, 4, 7)):
                v.tensor_scalar(c.mod[:, m, :], c.mod[:, m, :], 1.0, vec("L0_xcond_norm%s_w" % "1c2"[n]), ALU.add, ALU.mult)
            v.tensor_scalar(c.mod[:, 9, :], c.mod[:, 9, :], 1.0, None, ALU.add)
            v.tensor_scalar(c.mod[:, 11, :], c.mod[:, 11, :], 1.0, None, ALU.add)
            dve.wait_ge(made, 14)
            v.tensor_scalar(c.bp[:], c.ps_pj[1][:, 0:1], vec("L1_xcond_bp"), None, ALU.add).then_inc(ready, 1)

        @block.scalar
        def _(act):
            a = nc.scalar
            act.wait_ge(loads, n_loads[0])
            for x in range(2):
                src = c.wqkv[:, D * x:D * x + D].rearrange("p (h t e) -> p h t e", t=2, e=4)
                dst = c.wrot[:, x, :].rearrange("p (h t e) -> p h t e", t=2, e=4)
                for t in range(2):
                    a.activation(dst[:, :, t, :], src[:, :, 1 - t, :], ACT.Copy)
            act.wait_ge(cond_t, 2)
            a.activation(c.cond_t[:, 1, :], c.cond_t[:, 0, :], ACT.Exp, scale=-1.0).then_inc(silu_e, 1)

        @block.tensor
        def _(pe):
            t = nc.tensor
            pe.wait_ge(loads, n_loads[0])
            pe.wait_ge(ready, 1)
            t.transpose(c.ps_pj[1][:, 0:NVEC], c.vec_rows[:], c.eye[0:NVEC, 0:NVEC])
            t.transpose(c.ps_pj[0][:, 0:B], c.cond[:], c.eye[0:B, 0:B]).then_inc(psum_full, 1)
            t.transpose(c.ps_mt16[:, 0:S], c.mask_nat[:], c.eye_bf[:])
            t.transpose(c.ps_mt16[0:SC, S:2 * S], c.key_rows[:], c.eye_bf[:]).then_inc(mask_ps, 1)
            pe.wait_ge(cond_t, 2)
            for m in range(13):
                if m == 9:
                    pe.wait_ge(silu_d, 3)
                if m >= 2:
                    pe.wait_ge(copied, m - 1)
                w = c.ada_w[:, D * m:D * m + D] if m < 9 else c.wss[:, (m - 9) // 2, D * ((m - 9) % 2):D * ((m - 9) % 2) + D]
                t.matmul(c.ps_pj[m % 2][:, 0:B], w, c.cond_t[:, 0 if m < 9 else 1, :],
                         start=True, stop=True).then_inc(made, 1)
            pe.wait_ge(copied, 12)
            t.matmul(c.ps_pj[1][:, 0:1], c.wp_in[:], vec("L1_xcond_bkv", 1), start=True, stop=True).then_inc(made, 1)


def load_phase(nc, c, x, ctx_in, ctx):
    s = lambda n: ctx.enter_context(nc.semaphore(n))
    came = [s("ld_came0"), s("ld_came1")]
    turned_x, turned_c, kept_x, kept_c = s("ld_turned_x"), s("ld_turned_c"), s("ld_kept_x"), s("ld_kept_c")
    with nc.Block() as block:
        @block.sync
        def _(sp):
            def body(i, par):
                if not is_first(i) and not (isinstance(i, int) and i < 2):
                    sp.wait_ge(turned_c, i - 1)
                sp.dma_start(c.in_x[:, par], x[bass.ds(G * i, G)].rearrange("b s d -> s b d")).then_inc(came[par], 16)
                sp.dma_start(c.in_c[0:SC, par], ctx_in[bass.ds(G * i, G)].rearrange("b s d -> s b d")).then_inc(came[par], 16)
            body(0, 0)
            body(1, 1)
            with sp.Fori(1, NG // 2) as t:
                body(2 * t, 0)
                body(2 * t + 1, 1)

        def pairs(eng, body):
            body(0, 0, 0)
            body(1, 1, 0)
            with eng.Fori(1, NG // 2) as t:
                body(2 * t, 0, t)
                body(2 * t + 1, 1, t)

        @block.tensor
        def _(pe):
            def body(i, par, t):
                pe.wait_ge(came[par], 32 * (t + 1))
                if not isinstance(i, int):
                    pe.wait_ge(kept_x, i - 1)
                    pe.wait_ge(kept_c, i - 1)
                for b in range(G):
                    m = nc.tensor.transpose(c.ps_st[par][:, S * b:S * b + S], c.in_x[:, par, b, :], c.eye[:])
                m.then_inc(turned_x, 1)
                for b in range(G):
                    m = nc.tensor.transpose(c.ps_nat[par][:, SC * b:SC * b + SC], c.in_c[0:SC, par, b, :], c.eye[0:SC, 0:SC])
                m.then_inc(turned_c, 1)
            pairs(pe, body)

        @block.vector
        def _(dve):
            def body(i, par, t):
                dve.wait_ge(turned_x, i + 1)
                nc.vector.tensor_copy(c.xt[:, bass.ds(NT * i, NT)], c.ps_st[par][:]).then_inc(kept_x, 1)
            pairs(dve, body)

        @block.scalar
        def _(act):
            def body(i, par, t):
                act.wait_ge(turned_c, i + 1)
                nc.scalar.activation(c.ct[:, bass.ds(NC * i, NC)], c.ps_nat[par][:, 0:NC], ACT.Copy).then_inc(kept_c, 1)
            pairs(act, body)


def norm_phase(nc, c, name, src, dst, n, factor, shift, ctx):
    s = lambda x: ctx.enter_context(nc.semaphore(name + x))
    centred, squared, varied, rooted, inverted, normed = (s("_centred"), s("_squared"), s("_varied"), s("_rooted"),
                                                          s("_inverted"), s("_normed"))
    w = G * n
    with nc.Block() as block:
        @block.tensor
        def _(pe):
            def centre(i, par):
                if not (isinstance(i, int) and i < 2):
                    pe.wait_ge(normed, i - 1)
                nc.tensor.matmul(c.ps_st[par][:, 0:w], c.centre[:], src[:, bass.ds(w * i, w)], start=True, stop=True).then_inc(centred, 1)

            def body(i, par):
                if not is_last(i):
                    centre(i + 1, 1 - par)
                pe.wait_ge(squared, i + 1)
                if not (isinstance(i, int) and i < 2):
                    pe.wait_ge(rooted, i - 1)
                nc.tensor.matmul(c.ps_nat[par][:, 0:w], c.mean[:], c.sq[:, par, 0:w], start=True, stop=True).then_inc(varied, 1)
            centre(0, 0)
            for_groups(pe, body)

        @block.scalar
        def _(act):
            def body(i, par):
                act.wait_ge(centred, i + 1)
                if not (isinstance(i, int) and i < 2):
                    act.wait_ge(varied, i - 1)
                nc.scalar.activation(c.sq[:, par, 0:w], c.ps_st[par][:, 0:w], ACT.Square).then_inc(squared, 1)
                act.wait_ge(varied, i + 1)
                if not (isinstance(i, int) and i < 2):
                    act.wait_ge(inverted, i - 1)
                nc.scalar.activation(c.sd[:, par, 0:w], c.ps_nat[par][:, 0:w], ACT.Sqrt, bias=c.eps[:]).then_inc(rooted, 1)
            for_groups(act, body)

        @block.vector
        def _(dve):
            def body(i, par):
                dve.wait_ge(rooted, i + 1)
                nc.vector.reciprocal(c.rs[:, par, 0:w], c.sd[:, par, 0:w]).then_inc(inverted, 1)
                dve.wait_ge(inverted, i + 1)
                nc.vector.tensor_tensor(c.xn[:, par, 0:w], c.ps_st[par][:, 0:w], c.rs[:, par, 0:w], ALU.mult).then_inc(normed, 1)
                dve.wait_ge(normed, i + 1)
                for b in range(G):
                    nc.vector.tensor_scalar(dst[:, bass.ds(w * i + n * b, n)], c.xn[:, par, n * b:n * b + n],
                                            c.mod[:, factor, bass.ds(G * i + b, 1)], c.mod[:, shift, bass.ds(G * i + b, 1)],
                                            ALU.mult, ALU.add)
            for_groups(dve, body)


def attention_phase(nc, c, name, ctx, *, nk, kv_src, wq, wk, wv, wo, rotate=False, q_bias=None,
                    k_bias=None, pair_mask=False, key_mask=False, gate=None, out_bias=None):
    s = lambda x: ctx.enter_context(nc.semaphore(name + x))
    pj_full = s("_pj_full")
    pj_read_v = s("_pj_read_v")
    pj_read_a = s("_pj_read_a")
    turned = s("_turned")
    high, mid = s("_high"), s("_mid")
    rest, low = s("_rest"), s("_low")
    doubled = s("_doubled")
    biased = s("_biased")
    kv_here = s("_kv_here")
    stacked = [s("_stacked0"), s("_stacked1")]
    nat_full, maxed = s("_nat_full"), s("_maxed")
    max_split, max_turned, max_kept = s("_max_split"), s("_max_turned"), s("_max_kept")
    st_full, exped, pv_done = s("_st_full"), s("_exped"), s("_pv_done")
    inverted, out_ready = s("_inverted"), s("_out_ready")
    wo_full, added = s("_wo_full"), s("_added")
    NV = 4 if rotate else 2
    NP = NV + 1
    wk_cols = G * nk
    pitch = nk
    half = lambda hh: slice(64 * (hh % 2), 64 * (hh % 2) + 64)
    pair = lambda hh, g: 4 * (hh // 2) + g
    N_ADD = G if gate is not None else 1
    small = lambda i: isinstance(i, int)
    src_of = {"q": (c.ht, NT), "k": (kv_src, wk_cols), "v": (kv_src, wk_cols)}
    uses = ([("q", wq, 0), ("q", c.wrot[:, 0, :], 1), ("k", wk, 0), ("k", c.wrot[:, 1, :], 1)] if rotate
            else [("q", wq, 0), ("k", wk, 0)])

    with nc.Block() as block:
        @block.tensor
        def _(pe):
            t = nc.tensor

            def bank_free(i, u, par):
                v = u - 2
                if v >= 0:
                    group, use = i, v
                else:
                    group, use = i - 1, v + NP
                if small(group) and group < 0:
                    return
                if use < NV:
                    pe.wait_ge(pj_read_v, NV * group + use + 1)
                else:
                    pe.wait_ge(pj_read_a, group + 1)

            def project(i, par, u):
                bank = c.ps_pj[(par * NP + u) % 2]
                bank_free(i, u, par)
                if u < NV:
                    kind, w, _ = uses[u]
                    src, width = src_of[kind]
                    m = t.matmul(bank[:, 0:width], w, src[:, bass.ds(width * i, width)], start=True, stop=True)
                else:
                    pe.wait_ge(kv_here, i + 1)
                    for b in range(G):
                        m = t.matmul(bank[0:nk, D * b:D * b + D], c.kv_now[:, nk * b:nk * b + nk], wv,
                                     start=b == 0, stop=b == G - 1, skip_group_check=True)
                m.then_inc(pj_full, 1)

            def scores(i, par, j, hh):
                step = G * i + j
                if j == 0 and hh == 0:
                    pe.wait_ge(stacked[par], 256 * (pair_no(i, par) + 1))
                if not (small(step) and 4 * step + hh < 2):
                    pe.wait_ge(maxed, 4 * step + hh - 1)
                bank = c.ps_nat[hh % 2]
                kept = bank[:, 0:4 * pitch].rearrange("p (g k) -> p g k", g=4)[:, :, 0:nk]
                for g in range(4):
                    m = t.matmul(bank[:, pitch * g:pitch * g + pitch], c.qst[half(hh), par, pair(hh, g), S * j:S * j + S],
                                 c.kst[half(hh), par, pair(hh, g), nk * j:nk * j + pitch],
                                 start=g == 0, stop=g == 3, skip_group_check=True)
                if pair_mask:
                    m = t.matmul(kept, c.eye_bf[:], c.mask_nat[:].unsqueeze(1).broadcast_to([128, 4, nk]),
                                 start=False, stop=True, skip_group_check=True)
                if key_mask:
                    m = t.matmul(kept, c.eye_bf[:, bass.ds(G * i + j, 1)].broadcast_to([128, S]),
                                 c.key_rows[:].unsqueeze(1).broadcast_to([128, 4, nk]),
                                 start=False, stop=True, skip_group_check=True)
                m.then_inc(nat_full, 1)

            def turn_max(step):
                pe.wait_ge(max_split, 4 * step + 4)
                if not (small(step) and step < 1):
                    pe.wait_ge(max_kept, step)
                    pe.wait_ge(out_ready, step)
                t.transpose(c.ps_pomt[:, 256:320].bitcast(BF16), c.nm[:], c.eye_bf[:]).then_inc(max_turned, 1)

            def scores_t(i, par, j, hh):
                step = G * i + j
                if not (small(step) and 4 * step + hh < 2):
                    pe.wait_ge(exped, 4 * step + hh - 1)
                bank = c.ps_st[hh % 2]
                rows = half(hh)
                for g in range(4):
                    t.matmul(bank[0:nk, S * g:S * g + S], c.kst[rows, par, pair(hh, g), nk * j:nk * j + nk],
                             c.qst[rows, par, pair(hh, g), S * j:S * j + S], start=g == 0, stop=False, skip_group_check=True)
                if pair_mask:
                    t.matmul(bank[0:nk, :], c.eye_bf[:], c.mask_t[:].unsqueeze(1).broadcast_to([128, 4, S]),
                             start=False, stop=False, skip_group_check=True)
                if hh == 0:
                    pe.wait_ge(max_kept, step + 1)
                for g in range(4):
                    m = t.matmul(bank[0:nk, S * g:S * g + S], c.head_sel[rows, 4 * hh + g, 0:nk], c.mt[rows, j % 2, :],
                                 start=False, stop=g == 3, skip_group_check=True)
                m.then_inc(st_full, 1)

            def values(i, par, j, hh):
                step = G * i + j
                pe.wait_ge(exped, 4 * step + hh + 1)
                if hh == 0:
                    pe.wait_ge(pj_read_a, i + 1)
                for g in range(4):
                    out = c.ps_pomt[32 * g:32 * g + 32, :]
                    t.matmul(out[:, 0:S], c.vz[0:nk, par, j, g, 32 * hh:32 * hh + 32], c.p[0:nk, hh, S * g:S * g + S],
                             start=hh == 0, stop=hh == 3, skip_group_check=True)
                for g in range(4):
                    out = c.ps_pomt[32 * g:32 * g + 32, :]
                    m = t.matmul(out[:, S:2 * S], c.ones_z[0:nk, hh, :], c.p[0:nk, hh, S * g:S * g + S],
                                 start=False, stop=hh == 3, skip_group_check=True)
                m.then_inc(pv_done, 1)

            def project_out(i, par):
                pe.wait_ge(out_ready, G * i + G)
                if not (small(i) and i < 1):
                    pe.wait_ge(added, N_ADD * i)
                t.matmul(c.ps_wo[:], wo, c.ot[:, par, :], start=True, stop=True).then_inc(wo_full, 1)

            def body(i, par):
                for j in range(G):
                    if j < G - 1:
                        nxt = lambda hh, j=j: scores(i, par, j + 1, hh)
                    elif is_last(i):
                        nxt = lambda hh: None
                    else:
                        nxt = lambda hh: scores(i + 1, 1 - par, 0, hh)
                    todo = [] if is_last(i) else {0: range(0, NV), 1: range(NV, NP), 2: (), 3: ()}[j]
                    nxt(0)
                    nxt(1)
                    turn_max(G * i + j)
                    for u in todo:
                        project(i + 1, 1 - par, u)
                    scores_t(i, par, j, 0)
                    nxt(2)
                    scores_t(i, par, j, 1)
                    values(i, par, j, 0)
                    nxt(3)
                    scores_t(i, par, j, 2)
                    values(i, par, j, 1)
                    scores_t(i, par, j, 3)
                    values(i, par, j, 2)
                    if j == 0 and not is_first(i):
                        project_out(i - 1, 1 - par)
                    values(i, par, j, 3)

            for u in range(NP):
                project(0, 0, u)
            for hh in range(4):
                scores(0, 0, 0, hh)
            for_groups(pe, body)
            project_out(NG - 1, 1)

        @block.vector
        def _(dve):
            v = nc.vector

            def take(i, par, u):
                kind, _, half = uses[u]
                width = src_of[kind][1]
                x = 0 if kind == "q" else 1
                bank = c.ps_pj[(par * NP + u) % 2]
                dve.wait_ge(pj_full, NP * i + u + 1)
                if not (small(i) and i < 1):
                    dve.wait_ge(turned if rotate else low, 2 * (i - 1) + x + 1)
                if rotate:
                    table = ((c.cosq, c.sinq), (c.cos, c.sin))[x][half]
                    v.tensor_tensor(c.part[:, x, half, :].rearrange("p (r n) -> p r n", n=64),
                                    bank[:].rearrange("p (r n) -> p r n", n=64),
                                    table[:].unsqueeze(1).broadcast_to([128, 8, 64]), ALU.mult).then_inc(pj_read_v, 1)
                elif x == 0:
                    v.tensor_scalar(c.whole[:, x, 0:width], bank[:, 0:width], q_bias, SCALE, ALU.add, ALU.mult).then_inc(pj_read_v, 1)
                else:
                    v.tensor_scalar(c.whole[:, x, 0:width], bank[:, 0:width], k_bias, None, ALU.add).then_inc(pj_read_v, 1)

            def maxima(step, j):
                for hh in range(4):
                    dve.wait_ge(nat_full, 4 * step + hh + 1)
                    if hh == 0 and not (small(step) and step < 1):
                        dve.wait_ge(max_split, 4 * step)
                    v.tensor_reduce(c.negmax[:, 4 * hh:4 * hh + 4], c.ps_nat[hh % 2][:, 0:4 * pitch].rearrange("p (g k) -> p g k", g=4)[:, :, 0:nk],
                                    AX_X, ALU.max, negate=True).then_inc(maxed, 1)
                dve.wait_ge(maxed, 4 * step + 4)
                if not (small(step) and step < 1):
                    dve.wait_ge(max_turned, step)
                nm = c.nm[:].rearrange("p (r t h) -> p r t h", r=2, t=4)
                twice = lambda ap: ap.unsqueeze(1).broadcast_to([128, 2, H])
                v.tensor_copy(nm[:, :, 0, :], twice(c.negmax[:])).then_inc(max_split, 1)
                dve.wait_ge(max_split, 4 * step + 1)
                v.tensor_tensor(c.negrest[:], c.negmax[:], nm[:, 0, 0, :], ALU.subtract).then_inc(max_split, 1)
                dve.wait_ge(max_split, 4 * step + 2)
                v.tensor_copy(nm[:, :, 1, :], twice(c.negrest[:])).then_inc(max_split, 1)
                dve.wait_ge(max_split, 4 * step + 3)
                v.tensor_tensor(nm[:, :, 2, :], twice(c.negrest[:]), nm[:, :, 1, :], ALU.subtract).then_inc(max_split, 1)

            def double(i, x, which):
                width = NT if x == 0 else wk_cols
                slots = (HIGH if which == 0 else MID)[x]
                dve.wait_ge(high if which == 0 else mid, 2 * i + x + 1)
                for to in slots[1:]:
                    v.tensor_copy(c.parts[:, x, to, 0:width], c.parts[:, x, slots[0], 0:width]).then_inc(doubled, 1)

            def normalise(i, par, j):
                step = G * i + j
                dve.wait_ge(pv_done, 4 * step + 4)
                v.reciprocal(c.rden[:], c.ps_pomt[:, S:2 * S]).then_inc(inverted, 1)
                dve.wait_ge(inverted, step + 1)
                if j == 0 and not (small(i) and i < 2):
                    dve.wait_ge(wo_full, i - 1)
                v.tensor_tensor(c.ot[:, par, S * j:S * j + S], c.ps_pomt[:, 0:S], c.rden[:], ALU.mult).then_inc(out_ready, 1)

            def add_out(i):
                dve.wait_ge(wo_full, i + 1)
                if gate is None:
                    xs = c.xt[:, bass.ds(NT * i, NT)]
                    v.scalar_tensor_tensor(out=xs, in0=c.ps_wo[:], scalar=out_bias, in1=xs, op0=ALU.add, op1=ALU.add).then_inc(added, 1)
                else:
                    for b in range(G):
                        xs = c.xt[:, bass.ds(NT * i + S * b, S)]
                        v.scalar_tensor_tensor(out=xs, in0=c.ps_wo[:, S * b:S * b + S], scalar=c.mod[:, gate, bass.ds(G * i + b, 1)],
                                               in1=xs, op0=ALU.mult, op1=ALU.add).then_inc(added, 1)

            def body(i, par):
                for j in range(G):
                    if j == 0 and not is_last(i):
                        for u in range(NV):
                            take(i + 1, 1 - par, u)
                    if j in (1, 2) and not is_last(i):
                        double(i + 1, 0, j - 1)
                        double(i + 1, 1, j - 1)
                    if not (is_last(i) and j == G - 1):
                        maxima(G * i + j + 1, j + 1)
                    if j == 0 and not is_first(i):
                        add_out(i - 1)
                    normalise(i, par, j)
                    if key_mask and j == 0 and not is_last(i):
                        v.tensor_copy(c.bias_now[0:nk, 1 - par, :], c.key_bias[0:nk, bass.ds(G * (i + 1), G)]).then_inc(biased, 1)

            if key_mask:
                v.tensor_copy(c.bias_now[0:nk, 0, :], c.key_bias[0:nk, 0:G]).then_inc(biased, 1)
            for u in range(NV):
                take(0, 0, u)
            for which in range(2):
                for x in range(2):
                    double(0, x, which)
            maxima(0, 0)
            for_groups(dve, body)
            add_out(NG - 1)

        @block.scalar
        def _(act):
            a = nc.scalar

            def split_high(i, par, x):
                width = NT if x == 0 else wk_cols
                act.wait_ge(turned if rotate else pj_read_v, 2 * i + x + 1)
                if not (small(i) and i < 1):
                    act.wait_ge(stacked[1 - par], 256 * pair_no(i - 1, 1 - par) + 128 * x + 128)
                a.activation(c.parts[:, x, HIGH[x][0], 0:width], c.whole[:, x, 0:width], ACT.Copy).then_inc(high, 1)

            def split_mid(i, x):
                width = NT if x == 0 else wk_cols
                act.wait_ge(rest, 2 * i + x + 1)
                a.activation(c.parts[:, x, MID[x][0], 0:width], c.whole[:, x, 0:width], ACT.Copy).then_inc(mid, 1)

            def take_values(i, par):
                act.wait_ge(pj_full, NP * i + NP)
                if not (small(i) and i < 2):
                    act.wait_ge(pv_done, 16 * (i - 1))
                for hh in range(4):
                    src = c.ps_pj[(par * NP + NV) % 2][0:nk, :].rearrange("p (b t f) -> p b t f", b=G, t=H // 2)
                    m = a.activation(c.vz[0:nk, par, :, :, 40 * hh:40 * hh + HD],
                                     src[:, :, pair(hh, 0):pair(hh, 0) + 4, HD * (hh % 2):HD * (hh % 2) + HD], ACT.Copy)
                m.then_inc(pj_read_a, 1)

            def keep_max(step, j):
                act.wait_ge(max_turned, step + 1)
                if not (small(step) and step < 2):
                    act.wait_ge(st_full, 4 * (step - 1))
                a.activation(c.mt[:, j % 2, :], c.ps_pomt[:, 256:320].bitcast(BF16), ACT.Copy).then_inc(max_kept, 1)

            def exponentials(i, par, j, hh):
                step = G * i + j
                act.wait_ge(st_full, 4 * step + hh + 1)
                if not (small(step) and step < 1):
                    act.wait_ge(pv_done, 4 * (step - 1) + hh + 1)
                if key_mask and j == 0 and hh == 0:
                    act.wait_ge(biased, i + 1)
                bias = c.bias_now[0:nk, par, j:j + 1] if key_mask else 0.0
                a.activation(c.p[0:nk, hh, :], c.ps_st[hh % 2][0:nk, :], ACT.Exp, bias=bias).then_inc(exped, 1)

            def body(i, par):
                for j in range(G):
                    keep_max(G * i + j, j)
                    exponentials(i, par, j, 0)
                    exponentials(i, par, j, 1)
                    if not is_last(i):
                        if j == 0:
                            split_high(i + 1, 1 - par, 0)
                        if j == 1:
                            split_mid(i + 1, 0)
                            split_mid(i + 1, 1)
                        if j == 2:
                            take_values(i + 1, 1 - par)
                    exponentials(i, par, j, 2)
                    exponentials(i, par, j, 3)
                    if j == 0 and not is_last(i):
                        split_high(i + 1, 1 - par, 1)

            split_high(0, 0, 0)
            split_high(0, 0, 1)
            split_mid(0, 0)
            split_mid(0, 1)
            take_values(0, 0)
            for_groups(act, body)

        @block.gpsimd
        def _(pool):
            def body(i, par):
                if not (small(i) and i < 1):
                    pool.wait_ge(pj_full, NP * i)
                nc.gpsimd.tensor_copy(c.kv_now[:, 0:wk_cols], kv_src[:, bass.ds(wk_cols * i, wk_cols)]).then_inc(kv_here, 1)
                if rotate:
                    for x in range(2):
                        pool.wait_ge(pj_read_v, NV * i + 2 * x + 2)
                        if not (small(i) and i < 1):
                            pool.wait_ge(low, 2 * (i - 1) + x + 1)
                        nc.gpsimd.tensor_tensor(c.whole[:, x, :], c.part[:, x, 0, :], c.part[:, x, 1, :], ALU.add).then_inc(turned, 1)
                for x in range(2):
                    w = slice(0, NT if x == 0 else wk_cols)
                    pool.wait_ge(high, 2 * i + x + 1)
                    nc.gpsimd.tensor_tensor(c.whole[:, x, w], c.whole[:, x, w], c.parts[:, x, HIGH[x][0], w], ALU.subtract).then_inc(rest, 1)
                for x in range(2):
                    w = slice(0, NT if x == 0 else wk_cols)
                    pool.wait_ge(mid, 2 * i + x + 1)
                    nc.gpsimd.tensor_tensor(c.parts[:, x, LOW[x], w], c.whole[:, x, w], c.parts[:, x, MID[x][0], w], ALU.subtract).then_inc(low, 1)
            for_groups(pool, body)

        @block.sync
        def _(sp):
            def body(i, par):
                number = (lambda v: v) if small(i) else sp.snap
                split = [number(2 * i + 1), number(2 * i + 2)]
                copied = number(6 * i + 6)
                used = number(16 * (i - 1))
                for x in range(2):
                    width = NT if x == 0 else wk_cols
                    st = c.qst if x == 0 else c.kst
                    if x == 0:
                        if not (small(i) and i < 2):
                            sp.wait_ge(st_full, used)
                        sp.wait_ge(doubled, copied)
                    sp.wait_ge(low, split[x])
                    for t in range(H // 2):
                        sp.dma_start(st[:, par, t, 0:width], c.parts[16 * t:16 * t + 16, x, :, 0:width]).then_inc(stacked[par], 16)
            for_groups(sp, body)


def pair_no(i, par):
    if isinstance(i, int):
        return i // 2
    return (i - par) // 2


def mlp_phase(nc, c, ctx):
    s = lambda x: ctx.enter_context(nc.semaphore("mlp" + x))
    up_full, gelued, down_full, gated, added = s("_up_full"), s("_gelued"), s("_down_full"), s("_gated"), s("_added")
    NF = F // 128
    with nc.Block() as block:
        @block.tensor
        def _(pe):
            banks = [c.ps_nat[0], c.ps_nat[1], c.ps_st[0], c.ps_st[1]]

            def up(i, f):
                if not (isinstance(i, int) and i < 1):
                    pe.wait_ge(gelued, NF * (i - 1) + f + 1)
                nc.tensor.matmul(banks[f][:], c.w1[:, 128 * f:128 * f + 128], c.ht[:, bass.ds(NT * i, NT)], start=True, stop=True).then_inc(up_full, 1)

            def body(i, par):
                if not (isinstance(i, int) and i < 2):
                    pe.wait_ge(gated, G * (i - 1))
                for f in range(NF):
                    if not is_last(i):
                        up(i + 1, f)
                    pe.wait_ge(gelued, NF * i + f + 1)
                    m = nc.tensor.matmul(c.ps_pj[par][:], c.w2[:, f, :], c.hid[par][f], start=f == 0, stop=f == NF - 1)
                m.then_inc(down_full, 1)
            for f in range(NF):
                up(0, f)
            for_groups(pe, body)

        @block.scalar
        def _(act):
            banks = [c.ps_nat[0], c.ps_nat[1], c.ps_st[0], c.ps_st[1]]

            def body(i, par):
                if not (isinstance(i, int) and i < 2):
                    act.wait_ge(down_full, i - 1)
                for f in range(NF):
                    act.wait_ge(up_full, NF * i + f + 1)
                    nc.scalar.activation(c.hid[par][f], banks[f][:], ACT.Gelu_apprx_tanh, bias=c.vec[:, c.vec_row["L0_xcond_mlp_b1"] + f:c.vec_row["L0_xcond_mlp_b1"] + f + 1]).then_inc(gelued, 1)
            for_groups(act, body)

        @block.vector
        def _(dve):
            def body(i, par):
                dve.wait_ge(down_full, i + 1)
                if not (isinstance(i, int) and i < 2):
                    dve.wait_ge(added, i - 1)
                for b in range(G):
                    nc.vector.tensor_scalar(c.xn[:, par, S * b:S * b + S], c.ps_pj[par][:, S * b:S * b + S], c.vec[:, c.vec_row["L0_xcond_mlp_b2"]:c.vec_row["L0_xcond_mlp_b2"] + 1],
                                            c.mod[:, 8, bass.ds(G * i + b, 1)], ALU.add, ALU.mult).then_inc(gated, 1)
            for_groups(dve, body)

        @block.gpsimd
        def _(pool):
            def body(i, par):
                pool.wait_ge(gated, G * (i + 1))
                xs = c.xt[:, bass.ds(NT * i, NT)]
                nc.gpsimd.tensor_tensor(xs, xs, c.xn[:, par, :], ALU.add).then_inc(added, 1)
            for_groups(pool, body)


def store_phase(nc, c, out, ctx):
    s = lambda x: ctx.enter_context(nc.semaphore("out" + x))
    fetched, turned, copied = s("_fetched"), s("_turned"), s("_copied")
    stored = [s("_stored0"), s("_stored1")]
    with nc.Block() as block:
        @block.scalar
        def _(act):
            def body(i, par):
                if not (isinstance(i, int) and i < 2):
                    act.wait_ge(turned, i - 1)
                nc.scalar.activation(c.ot[:, par, :], c.xt[:, bass.ds(NT * i, NT)], ACT.Copy).then_inc(fetched, 1)
            for_groups(act, body)

        @block.tensor
        def _(pe):
            def body(i, par):
                pe.wait_ge(fetched, i + 1)
                if not (isinstance(i, int) and i < 2):
                    pe.wait_ge(copied, i - 1)
                for b in range(G):
                    m = nc.tensor.transpose(c.ps_st[par][:, S * b:S * b + S], c.ot[:, par, S * b:S * b + S], c.eye[:])
                m.then_inc(turned, 1)
            for_groups(pe, body)

        @block.vector
        def _(dve):
            def body(i, par):
                dve.wait_ge(turned, i + 1)
                if not (isinstance(i, int) and i < 2):
                    dve.wait_ge(stored[par], 16 * pair_no(i, par))
                nc.vector.tensor_copy(c.in_x[:, par].rearrange("p b d -> p (b d)"), c.ps_st[par][:]).then_inc(copied, 1)
            for_groups(dve, body)

        @block.sync
        def _(sp):
            def body(i, par):
                sp.wait_ge(copied, i + 1)
                sp.dma_start(out[bass.ds(G * i, G)].rearrange("b s d -> s b d"), c.in_x[:, par]).then_inc(stored[par], 16)
            for_groups(sp, body)
            sp.wait_ge(stored[0], 16 * NG // 2)
            sp.wait_ge(stored[1], 16 * NG // 2)


def two_layers(nc, ins, out):
    with ExitStack() as ctx:
        c = Core()

        def sb(name, shape, dt=F32):
            return ctx.enter_context(nc.sbuf_tensor(name, shape, dt))

        c.xt = sb("xt", [D, B * S])
        c.ht = sb("ht", [D, B * S])
        c.ct = sb("ct", [D, B * SC])
        c.wqkv = sb("wqkv", [D, 3 * D])
        c.wrot = sb("wrot", [D, 2, D])
        c.w0 = sb("w0", [D, 5, D])
        c.w1 = sb("w1", [D, F])
        c.w2 = sb("w2", [128, F // 128, D])
        c.wq = sb("wq", [D, D])
        c.wkv = sb("wkv", [D, 2 * D])
        c.wp = sb("wp", [D, D])
        c.vec = sb("vec", [128, NVEC])
        c.bp = sb("bp", [128, 1])
        c.cos = sb("cos", [128, 64])
        c.sin = sb("sin", [128, 64])
        c.cosq = sb("cosq", [128, 64])
        c.sinq = sb("sinq", [128, 64])
        c.mask8 = sb("mask8", [S, S], U8)
        c.key8 = sb("key8", [128, SC], U8)
        c.mask_nat = sb("mask_nat", [S, S], BF16)
        c.mask_t = sb("mask_t", [S, S], BF16)
        c.key_bias = sb("key_bias", [128, B])
        c.bias_now = sb("bias_now", [128, 2, G])
        c.key_rows = sb("key_rows", [128, SC], BF16)
        c.eye = sb("eye", [128, 128])
        c.eye_bf = sb("eye_bf", [128, 128], BF16)
        c.pick = sb("pick", [128, H])
        c.head_sel = sb("head_sel", [128, H, S], BF16)
        c.mean = sb("mean", [D, D])
        c.centre = sb("centre", [D, D])
        c.eps = sb("eps", [128, 1])
        c.ones_z = sb("ones_z", [128, 4, 32])
        c.mod = sb("mod", [D, 13, B])
        c.part = sb("part", [D, 2, 2, NT])
        c.whole = sb("whole", [D, 2, NT])
        c.parts = sb("parts", [D, 2, SLOTS, NT], BF16)
        c.qst = sb("qst", [128, 2, H // 2, NT], BF16)
        c.kst = sb("kst", [128, 2, H // 2, NT], BF16)
        c.vz = sb("vz", [128, 2, G, 4, 160])
        c.p = sb("p", [128, 4, NT])
        c.kv_now = sb("kv_now", [D, NT])
        c.negmax = sb("negmax", [S, H])
        c.nm = sb("nm", [S, 128], BF16)
        c.negrest = sb("negrest", [S, H])
        c.mt = sb("mt", [128, 2, S], BF16)
        c.rden = sb("rden", [D, S])
        c.ot = sb("ot", [D, 2, NT])
        c.hid = [[c.part[:, 0, 0], c.part[:, 0, 1], c.part[:, 1, 0], c.part[:, 1, 1]],
                 [c.whole[:, 0], c.whole[:, 1], c.p[:, 2], c.p[:, 3]]]
        c.sq, c.sd, c.rs, c.xn = c.part[:, 0], c.part[:, 1], c.whole[:], c.p[:, 0:2]
        c.in_x = c.p[:, 0:2].rearrange("p a (b d) -> p a b d", d=D)
        c.in_c = c.p[:, 2:4].rearrange("p a (b d) -> p a b d", d=D)
        c.ada_w = c.ht[:, 0:9 * D]
        c.wss = c.ht[:, 9 * D:13 * D].rearrange("p (a n) -> p a n", a=2)
        c.wp_in = c.ht[:, 16 * D:17 * D]
        c.cond = c.ht[0:B, 17 * D:18 * D]
        c.cond_t = c.ht[:, 18 * D:19 * D].rearrange("p (a b) -> p a b", a=2)
        c.vec_rows = c.ht[0:NVEC, 19 * D:20 * D]
        ps = lambda name, dt=F32: ctx.enter_context(nc.psum_tensor(name, [128, 512], dt))
        c.vec_row = VEC_ROW
        c.ps_nat = [ps("ps_nat0"), ps("ps_nat1")]
        c.ps_st = [ps("ps_st0"), ps("ps_st1")]
        c.ps_pj = [ps("ps_pj0"), ps("ps_pj1")]
        c.ps_pomt = ps("ps_pomt")
        c.ps_wo = ps("ps_wo")
        c.ps_mt16 = c.ps_wo[:].bitcast(BF16)

        setup_phase(nc, c, ins, ctx)
        load_phase(nc, c, ins["x"], ins["ctx_1024"], ctx)
        norm_phase(nc, c, "n1", c.xt, c.ht, S, 1, 0, ctx)
        attention_phase(nc, c, "sa", ctx, nk=S, kv_src=c.ht, wq=c.wqkv[:, 0:D], wk=c.wqkv[:, D:2 * D], wv=c.wqkv[:, 2 * D:3 * D],
                        wo=c.w0[:, 0, :], rotate=True, pair_mask=True, gate=2)
        norm_phase(nc, c, "n2", c.xt, c.ht, S, 4, 3, ctx)
        attention_phase(nc, c, "ca", ctx, nk=SC, kv_src=c.ct, wq=c.w0[:, 1, :], wk=c.w0[:, 2, :], wv=c.w0[:, 3, :], wo=c.w0[:, 4, :],
                        q_bias=0.0, k_bias=0.0, key_mask=True, gate=5)
        norm_phase(nc, c, "n3", c.xt, c.ht, S, 7, 6, ctx)
        mlp_phase(nc, c, ctx)
        norm_phase(nc, c, "n4", c.xt, c.ht, S, 9, 10, ctx)
        norm_phase(nc, c, "n5", c.ct, c.ct, SC, 11, 12, ctx)
        attention_phase(nc, c, "xa", ctx, nk=SC, kv_src=c.ct, wq=c.wq[:], wk=c.wkv[:, 0:D], wv=c.wkv[:, D:2 * D], wo=c.wp[:],
                        q_bias=c.vec[:, VEC_ROW["L1_xcond_bq"]:VEC_ROW["L1_xcond_bq"] + 1],
                        k_bias=c.vec[:, VEC_ROW["L1_xcond_bkv"]:VEC_ROW["L1_xcond_bkv"] + 1], out_bias=c.bp[:, 0:1])
        store_phase(nc, c, out, ctx)


def rope_tables():
    n = 64
    inv = 1.0 / 10000.0 ** (np.arange(0, HD, 2, dtype=np.float32) / HD)
    freqs = np.outer(np.arange(n, dtype=np.float32), inv)
    emb = np.concatenate([freqs, freqs], axis=-1)
    cos, sin = np.cos(emb).astype(np.float32), np.sin(emb).astype(np.float32)
    sin[:, :HD // 2] *= -1
    return np.ascontiguousarray(np.tile(cos.T, (H, 1))), np.ascontiguousarray(np.tile(sin.T, (H, 1)))


_INS = ["x", "cond_1024", "ctx_1024", "mask_BxS2_bf1", "mask_SxS_bk0"] + ["L0_xcond_" + n for n in (
    "adaLN_W", "adaLN_b", "norm1_w", "qkv_W", "attn_out_W", "normc_w", "cq_W", "ck_W", "cv_W", "co_W", "norm2_w",
    "mlp_W1", "mlp_b1", "mlp_W2", "mlp_b2")] + ["L1_xcond_" + n for n in (
        "Wq", "bq", "Wkv", "bkv", "Wp", "bp", "Wss_q", "bss_q", "Wss_kv", "bss_kv")]


def kernel(**inputs):
    import concourse.bacc as _bacc
    from concourse.bass_utils import run_bass_kernel_spmd as _run

    nc = _bacc.Bacc("TRN2", target_bir_lowering=False, num_devices=1)
    cos, sin = rope_tables()
    arrays, args = {}, {}

    def give(name, a):
        a = np.ascontiguousarray(a)
        if a.dtype == np.bool_:
            a = a.view(np.uint8 if a.shape[-1] % 4 else np.int32)
        arrays[f"in_{name}_dram"] = a
        args[name] = nc.dram_tensor(f"in_{name}_dram", a.shape, mybir.dt.from_np(a.dtype), kind="ExternalInput").ap()

    for name in _INS:
        give(name, inputs[name])
    give("cos", cos)
    give("sin", sin)
    out = nc.dram_tensor("out_0_dram", (B, S, D), F32, kind="ExternalOutput").ap()
    two_layers(nc, args, out)
    r = _run(nc, [arrays], core_ids=[0])
    return r.results[0]["out_0_dram"]
```

```python
from contextlib import ExitStack

import numpy as np
import concourse.bass as bass
from concourse import mybir

F32 = mybir.dt.float32
F32R = mybir.dt.float32r
BF16 = mybir.dt.bfloat16
U8 = mybir.dt.uint8
ALU = mybir.AluOpType
ACT = mybir.ActivationFunctionType
AX_X = mybir.AxisListType.X

B, S, D = 64, 128, 128
SC = 77
H, HD = 16, 8
G = 4
NG = B // G
NT, NC = G * S, G * SC
F = 4 * D
EPS = 1e-5
SCALE = 1.0 / float(np.sqrt(HD))
BIG = 2.0 ** 126
HIGH = ((0, 1, 2), (0, 3, 5))
MID = ((3, 4), (1, 4))
LOW = (5, 2)
SLOTS = 8


VEC_ROW = {"L0_xcond_adaLN_b": 0, "L1_xcond_bss_q": 9, "L1_xcond_bss_kv": 11, "L0_xcond_norm1_w": 13,
           "L0_xcond_normc_w": 14, "L0_xcond_norm2_w": 15, "L0_xcond_mlp_b2": 16, "L1_xcond_bq": 17, "L1_xcond_bp": 18,
           "L0_xcond_mlp_b1": 19, "L1_xcond_bkv": 23}
NVEC = 25


def for_groups(eng, body):
    body(0, 0)
    with eng.Fori(0, (NG - 2) // 2) as t:
        body(2 * t + 1, 1)
        body(2 * t + 2, 0)
    body(NG - 1, 1)


class Core:
    pass


def is_first(i):
    return isinstance(i, int) and i == 0


def is_last(i):
    return isinstance(i, int) and i == NG - 1


def wait_past(eng, sem, value, i, behind=0):
    if isinstance(value, int) and value <= 0:
        return
    eng.wait_ge(sem, value)


def setup_phase(nc, c, ins, ctx):
    s = lambda n: ctx.enter_context(nc.semaphore(n))
    loads = s("su_loads")
    zeroed, eyed, ready = s("su_zeroed"), s("su_eyed"), s("su_ready")
    psum_full, cond_t, silu_e, silu_d, copied = (s("su_psum_full"), s("su_cond_t"), s("su_silu_e"),
                                                 s("su_silu_d"), s("su_copied"))
    made, masks, mask_ps = s("su_made"), s("su_masks"), s("su_mask_ps")
    steps = s("su_steps")
    n_loads = [0]
    vec = lambda name, n=0: c.vec[:, c.vec_row[name] + n:c.vec_row[name] + n + 1]
    with nc.Block() as block:
        @block.sync
        def _(sp):
            def load(dst, src):
                sp.dma_start(dst, src).then_inc(loads, 16)
                n_loads[0] += 16
            load(c.cond[:], ins["cond_1024"])
            load(c.ada_w[:], ins["L0_xcond_adaLN_W"])
            load(c.wqkv[:], ins["L0_xcond_qkv_W"])
            for n, name in enumerate(("cq_W", "ck_W", "cv_W")):
                load(c.w0[:, n + 1, :], ins["L0_xcond_" + name])
            load(c.w1[:], ins["L0_xcond_mlp_W1"])
            load(c.w2[:], ins["L0_xcond_mlp_W2"].rearrange("(f p) n -> p f n", p=128))
            load(c.wq[:], ins["L1_xcond_Wq"])
            load(c.wkv[:], ins["L1_xcond_Wkv"])
            load(c.wp_in[:], ins["L1_xcond_Wp"])
            for dst, name in ((c.w0[:, 0, :], "L0_xcond_attn_out_W"), (c.w0[:, 4, :], "L0_xcond_co_W"), (c.wp[:], "L1_xcond_Wp")):
                rows = ins[name].rearrange("(cc g e) n -> cc g e n", cc=2, g=4)
                for g in range(4):
                    for cc in range(2):
                        load(dst[32 * g + 16 * cc:32 * g + 16 * cc + 16, :], rows[cc, g])
            load(c.wss[:, 0, :], ins["L1_xcond_Wss_q"])
            load(c.wss[:, 1, :], ins["L1_xcond_Wss_kv"])
            for name, first in c.vec_row.items():
                n = ins[name].shape[0] // 128
                load(c.vec_rows[first:first + n, :], ins[name].rearrange("(c p) -> c p", p=128))
            load(c.cos[:], ins["cos"])
            load(c.sin[:], ins["sin"])
            load(c.mask8[:].bitcast(mybir.dt.int32), ins["mask_SxS_bk0"])
            load(c.key8[0:B, :], ins["mask_BxS2_bf1"])

        @block.gpsimd
        def _(pool):
            nc.gpsimd.memset(c.eye[:], 0.0).then_inc(zeroed, 1)
            nc.gpsimd.memset(c.pick[:], 0.0).then_inc(zeroed, 1)
            pool.wait_ge(zeroed, 2)
            nc.gpsimd.affine_select(out=c.eye[:], in_=c.eye[:], compare_op=ALU.not_equal, fill=1.0,
                                    base=0, pattern=[[-1, 128]], channel_multiplier=1).then_inc(eyed, 1)
            for n, a in enumerate((0, 1, 2, 4, 5, 6)):
                nc.gpsimd.affine_select(out=c.pick[:], in_=c.pick[:], compare_op=ALU.not_equal,
                                        fill=1.0, base=-16 * a, pattern=[[-1, 16]],
                                        channel_multiplier=1).then_inc(eyed, 1)
                pool.wait_ge(eyed, n + 2)

        @block.vector
        def _(dve):
            v = nc.vector
            v.memset(c.mean[:], 1.0 / D)
            v.memset(c.key_rows[:], 0.0)
            v.memset(c.eps[:], EPS)
            v.memset(c.vz[:], 0.0)
            v.memset(c.parts[:], 0.0)
            v.memset(c.nm[:], 0.0)
            v.memset(c.ones_z[:], 0.0).then_inc(steps, 1)
            dve.wait_ge(steps, 1)
            for hh in range(4):
                v.memset(c.ones_z[:, hh, HD * hh:HD * hh + HD], 1.0)
            dve.wait_ge(eyed, 7)
            v.tensor_scalar(c.centre[:], c.eye[:], -1.0 / D, None, ALU.add)
            v.tensor_copy(c.eye_bf[:], c.eye[:])
            v.tensor_copy(c.head_sel[:], c.pick[:].unsqueeze(2).broadcast_to([128, H, S]))
            dve.wait_ge(loads, n_loads[0])
            v.tensor_scalar(c.mask_nat[:], c.mask8[:], -1.0, BIG, ALU.add, ALU.mult).then_inc(masks, 1)
            v.tensor_scalar(c.key_rows[0:B, :], c.key8[0:B, :], -1.0, BIG, ALU.add, ALU.mult)
            v.tensor_scalar(c.cosq[:], c.cos[:], SCALE, None, ALU.mult)
            v.tensor_scalar(c.sinq[:], c.sin[:], SCALE, None, ALU.mult).then_inc(ready, 1)
            dve.wait_ge(psum_full, 1)
            v.tensor_copy(c.vec[:], c.ps_pj[1][:, 0:NVEC]).then_inc(cond_t, 1)
            v.tensor_copy(c.cond_t[:, 0, :], c.ps_pj[0][:, 0:B]).then_inc(cond_t, 1)
            dve.wait_ge(silu_e, 1)
            v.tensor_scalar(c.cond_t[:, 1, :], c.cond_t[:, 1, :], 1.0, None, ALU.add).then_inc(silu_d, 1)
            dve.wait_ge(silu_d, 1)
            v.reciprocal(c.cond_t[:, 1, :], c.cond_t[:, 1, :]).then_inc(silu_d, 1)
            dve.wait_ge(silu_d, 2)
            v.tensor_tensor(c.cond_t[:, 1, :], c.cond_t[:, 0, :], c.cond_t[:, 1, :], ALU.mult).then_inc(silu_d, 1)
            dve.wait_ge(mask_ps, 1)
            v.tensor_copy(c.mask_t[:], c.turned_mask[:, 0:S])
            v.tensor_copy(c.key_bias[0:SC, :], c.turned_mask[0:SC, S:S + B])
            for m in range(13):
                dve.wait_ge(made, m + 1)
                bias = c.vec[:, m:m + 1]
                v.tensor_scalar(c.mod[:, m, :], c.ps_pj[m % 2][:, 0:B], bias, None, ALU.add).then_inc(copied, 1)
            dve.wait_ge(copied, 13)
            for n, m in enumerate((1, 4, 7)):
                v.tensor_scalar(c.mod[:, m, :], c.mod[:, m, :], 1.0, vec("L0_xcond_norm%s_w" % "1c2"[n]), ALU.add, ALU.mult)
            v.tensor_scalar(c.mod[:, 9, :], c.mod[:, 9, :], 1.0, None, ALU.add)
            v.tensor_scalar(c.mod[:, 11, :], c.mod[:, 11, :], 1.0, None, ALU.add)
            dve.wait_ge(made, 14)
            v.tensor_scalar(c.bp[:], c.ps_pj[1][:, 0:1], vec("L1_xcond_bp"), None, ALU.add).then_inc(ready, 1)

        @block.scalar
        def _(act):
            a = nc.scalar
            act.wait_ge(loads, n_loads[0])
            for x in range(2):
                src = c.wqkv[:, D * x:D * x + D].rearrange("p (h t e) -> p h t e", t=2, e=4)
                dst = c.wrot[:, x, :].rearrange("p (h t e) -> p h t e", t=2, e=4)
                for t in range(2):
                    a.activation(dst[:, :, t, :], src[:, :, 1 - t, :], ACT.Copy)
            act.wait_ge(cond_t, 2)
            a.activation(c.cond_t[:, 1, :], c.cond_t[:, 0, :], ACT.Exp, scale=-1.0).then_inc(silu_e, 1)

        @block.tensor
        def _(pe):
            t = nc.tensor
            pe.wait_ge(loads, n_loads[0])
            pe.wait_ge(ready, 1)
            t.transpose(c.ps_pj[1][:, 0:NVEC], c.vec_rows[:], c.eye[0:NVEC, 0:NVEC])
            t.transpose(c.ps_pj[0][:, 0:B], c.cond[:], c.eye[0:B, 0:B]).then_inc(psum_full, 1)
            t.transpose(c.turned_mask[:, 0:S], c.mask_nat[:], c.eye_bf[:])
            t.transpose(c.turned_mask[0:SC, S:2 * S], c.key_rows[:], c.eye_bf[:]).then_inc(mask_ps, 1)
            pe.wait_ge(cond_t, 2)
            for m in range(13):
                if m == 9:
                    pe.wait_ge(silu_d, 3)
                if m >= 2:
                    pe.wait_ge(copied, m - 1)
                w = c.ada_w[:, D * m:D * m + D] if m < 9 else c.wss[:, (m - 9) // 2, D * ((m - 9) % 2):D * ((m - 9) % 2) + D]
                t.matmul(c.ps_pj[m % 2][:, 0:B], w, c.cond_t[:, 0 if m < 9 else 1, :],
                         start=True, stop=True).then_inc(made, 1)
            pe.wait_ge(copied, 12)
            t.matmul(c.ps_pj[1][:, 0:1], c.wp_in[:], vec("L1_xcond_bkv", 1), start=True, stop=True).then_inc(made, 1)


def load_phase(nc, c, x, ctx_in, ctx):
    s = lambda n: ctx.enter_context(nc.semaphore(n))
    came = [s("ld_came0"), s("ld_came1")]
    turned_x, turned_c, kept_x, kept_c = s("ld_turned_x"), s("ld_turned_c"), s("ld_kept_x"), s("ld_kept_c")
    with nc.Block() as block:
        @block.sync
        def _(sp):
            def body(i, par):
                if not is_first(i) and not (isinstance(i, int) and i < 2):
                    sp.wait_ge(turned_c, i - 1)
                sp.dma_start(c.in_x[:, par], x[bass.ds(G * i, G)].rearrange("b s d -> s b d")).then_inc(came[par], 16)
                sp.dma_start(c.in_c[0:SC, par], ctx_in[bass.ds(G * i, G)].rearrange("b s d -> s b d")).then_inc(came[par], 16)
            body(0, 0)
            body(1, 1)
            with sp.Fori(1, NG // 2) as t:
                body(2 * t, 0)
                body(2 * t + 1, 1)

        def pairs(eng, body):
            body(0, 0, 0)
            body(1, 1, 0)
            with eng.Fori(1, NG // 2) as t:
                body(2 * t, 0, t)
                body(2 * t + 1, 1, t)

        @block.tensor
        def _(pe):
            def body(i, par, t):
                pe.wait_ge(came[par], 32 * (t + 1))
                if not isinstance(i, int):
                    pe.wait_ge(kept_x, i - 1)
                    pe.wait_ge(kept_c, i - 1)
                for b in range(G):
                    m = nc.tensor.transpose(c.ps_st[par][:, S * b:S * b + S], c.in_x[:, par, b, :], c.eye[:])
                m.then_inc(turned_x, 1)
                for b in range(G):
                    m = nc.tensor.transpose(c.ps_nat[par][:, SC * b:SC * b + SC], c.in_c[0:SC, par, b, :], c.eye[0:SC, 0:SC])
                m.then_inc(turned_c, 1)
            pairs(pe, body)

        @block.vector
        def _(dve):
            def body(i, par, t):
                dve.wait_ge(turned_x, i + 1)
                nc.vector.tensor_copy(c.xt[:, bass.ds(NT * i, NT)], c.ps_st[par][:]).then_inc(kept_x, 1)
            pairs(dve, body)

        @block.scalar
        def _(act):
            def body(i, par, t):
                act.wait_ge(turned_c, i + 1)
                nc.scalar.activation(c.ct[:, bass.ds(NC * i, NC)], c.ps_nat[par][:, 0:NC], ACT.Copy).then_inc(kept_c, 1)
            pairs(act, body)


def for_quads(eng, body):
    for n in range(4):
        body(n, n)
    with eng.Fori(1, NG // 4 - 1) as t:
        for n in range(4):
            body(4 * t + n, n)
    for n in range(4):
        body(NG - 4 + n, n)


def norm_phase(nc, c, name, src, dst, n, factor, shift, ctx):
    s = lambda x: ctx.enter_context(nc.semaphore(name + x))
    centred, squared, varied, logged, rooted, normed = (s("_centred"), s("_squared"), s("_varied"), s("_logged"),
                                                        s("_rooted"), s("_normed"))
    w = G * n
    AHEAD = 2
    banks = [c.ps_st[0], c.ps_st[1], c.ps_pj[0], c.ps_pj[1]]
    early = lambda i, m: isinstance(i, int) and i < m
    with nc.Block() as block:
        @block.tensor
        def _(pe):
            def centre(i, m):
                if not early(i, 4):
                    pe.wait_ge(normed, i - 3)
                nc.tensor.matmul(banks[m][:, 0:w], c.centre[:], src[:, bass.ds(w * i, w)], start=True, stop=True).then_inc(centred, 1)

            def body(i, m):
                if not (isinstance(i, int) and i + AHEAD >= NG):
                    centre(i + AHEAD, (m + AHEAD) % 4)
                pe.wait_ge(squared, i + 1)
                if not early(i, 2):
                    pe.wait_ge(logged, i - 1)
                nc.tensor.matmul(c.ps_nat[m % 2][:, 0:w], c.mean[:], c.sq[:, m % 2, 0:w], start=True, stop=True).then_inc(varied, 1)
            for i in range(AHEAD):
                centre(i, i)
            for_quads(pe, body)

        @block.scalar
        def _(act):
            def square(i, m):
                act.wait_ge(centred, i + 1)
                if not early(i, 2):
                    act.wait_ge(varied, i - 1)
                nc.scalar.activation(c.sq[:, m % 2, 0:w], banks[m][:, 0:w], ACT.Square).then_inc(squared, 1)

            def body(i, m):
                if not (isinstance(i, int) and i + 1 >= NG):
                    square(i + 1, (m + 1) % 4)
                act.wait_ge(varied, i + 1)
                nc.scalar.activation(c.sd[:, m % 2, 0:w], c.ps_nat[m % 2][:, 0:w], ACT.Ln, bias=c.eps[:]).then_inc(logged, 1)
                act.wait_ge(logged, i + 1)
                if not early(i, 2):
                    act.wait_ge(normed, i - 1)
                nc.scalar.activation(c.rs[:, m % 2, 0:w], c.sd[:, m % 2, 0:w], ACT.Exp, scale=-0.5).then_inc(rooted, 1)
            nc.scalar.preload_act_table_set("natural_log_exp_and_others")
            square(0, 0)
            for_quads(act, body)

        @block.vector
        def _(dve):
            def body(i, m):
                dve.wait_ge(rooted, i + 1)
                nc.vector.tensor_tensor(c.xn[:, m % 2, 0:w], banks[m][:, 0:w], c.rs[:, m % 2, 0:w], ALU.mult).then_inc(normed, 1)
                dve.wait_ge(normed, i + 1)
                for b in range(G):
                    nc.vector.tensor_scalar(dst[:, bass.ds(w * i + n * b, n)], c.xn[:, m % 2, n * b:n * b + n],
                                            c.mod[:, factor, bass.ds(G * i + b, 1)], c.mod[:, shift, bass.ds(G * i + b, 1)],
                                            ALU.mult, ALU.add)
            for_quads(dve, body)


def attention_phase(nc, c, name, ctx, *, nk, kv_src, wq, wk, wv, wo, rotate=False, q_bias=None,
                    k_bias=None, pair_mask=False, key_mask=False, gate=None, out_bias=None):
    s = lambda x: ctx.enter_context(nc.semaphore(name + x))
    pj_full = s("_pj_full")
    pj_read_v = s("_pj_read_v")
    pj_read_a = s("_pj_read_a")
    turned = s("_turned")
    high, mid = s("_high"), s("_mid")
    rest = s("_rest")
    low = [s("_low_q"), s("_low_k")]
    doubled = [s("_doubled_q"), s("_doubled_k")]
    biased = s("_biased")
    kv_here = s("_kv_here")
    stacked = [s("_stacked0"), s("_stacked1")]
    nat_full, maxed = s("_nat_full"), s("_maxed")
    max_split, max_turned, max_kept = s("_max_split"), s("_max_turned"), s("_max_kept")
    st_full, exped, pv_done = s("_st_full"), s("_exped"), s("_pv_done")
    inverted, out_ready = s("_inverted"), s("_out_ready")
    wo_full, added = s("_wo_full"), s("_added")
    NV = 4 if rotate else 2
    NP = NV + 1
    wk_cols = G * nk
    pitch = nk
    half = lambda hh: slice(64 * (hh % 2), 64 * (hh % 2) + 64)
    pair = lambda hh, g: 4 * (hh // 2) + g
    N_ADD = G if gate is not None else 1
    small = lambda i: isinstance(i, int)
    src_of = {"q": (c.ht, NT), "k": (kv_src, wk_cols), "v": (kv_src, wk_cols)}
    uses = ([("q", wq, 0), ("q", c.wrot[:, 0, :], 1), ("k", wk, 0), ("k", c.wrot[:, 1, :], 1)] if rotate
            else [("q", wq, 0), ("k", wk, 0)])

    with nc.Block() as block:
        @block.tensor
        def _(pe):
            t = nc.tensor

            def project(i, par, u):
                bank = c.ps_pj[u % 2]
                if u >= 2:
                    pe.wait_ge(pj_read_v, NV * i + u - 1)
                elif not (small(i) and i < 1):
                    if u == 0:
                        pe.wait_ge(pj_read_a, i)
                    else:
                        pe.wait_ge(pj_read_v, NV * i)
                if u < NV:
                    kind, w, _ = uses[u]
                    src, width = src_of[kind]
                    m = t.matmul(bank[:, 0:width], w, src[:, bass.ds(width * i, width)], start=True, stop=True)
                else:
                    pe.wait_ge(kv_here, i + 1)
                    for b in range(G):
                        m = t.matmul(bank[0:nk, D * b:D * b + D], c.kv_now[:, nk * b:nk * b + nk], wv,
                                     start=b == 0, stop=b == G - 1, skip_group_check=True)
                m.then_inc(pj_full, 1)

            def scores(i, par, j, hh):
                step = G * i + j
                if j == 0 and hh == 0:
                    pe.wait_ge(stacked[par], 256 * (pair_no(i, par) + 1))
                if not (small(step) and 4 * step + hh < 2):
                    pe.wait_ge(maxed, 4 * step + hh - 1)
                bank = c.ps_nat[hh % 2]
                kept = bank[:, 0:4 * pitch].rearrange("p (g k) -> p g k", g=4)[:, :, 0:nk]
                for g in range(4):
                    m = t.matmul(bank[:, pitch * g:pitch * g + pitch], c.qst[half(hh), par, pair(hh, g), S * j:S * j + S],
                                 c.kst[half(hh), par, pair(hh, g), nk * j:nk * j + pitch],
                                 start=g == 0, stop=g == 3, skip_group_check=True)
                if pair_mask:
                    m = t.matmul(kept, c.eye_bf[:], c.mask_nat[:].unsqueeze(1).broadcast_to([128, 4, nk]),
                                 start=False, stop=True, skip_group_check=True)
                if key_mask:
                    m = t.matmul(kept, c.eye_bf[:, bass.ds(G * i + j, 1)].broadcast_to([128, S]),
                                 c.key_rows[:].unsqueeze(1).broadcast_to([128, 4, nk]),
                                 start=False, stop=True, skip_group_check=True)
                m.then_inc(nat_full, 1)

            def turn_max(step, j):
                pe.wait_ge(max_split, 4 * step + 4)
                if not (small(step) and step < 2):
                    pe.wait_ge(out_ready, step - 1)
                t.transpose(c.turned_max[j % 2], c.nm[:], c.eye_bf[:]).then_inc(max_turned, 1)

            def scores_t(i, par, j, hh):
                step = G * i + j
                if not (small(step) and 4 * step + hh < 2):
                    pe.wait_ge(exped, 4 * step + hh - 1)
                bank = c.ps_st[hh % 2]
                rows = half(hh)
                for g in range(4):
                    t.matmul(bank[0:nk, S * g:S * g + S], c.kst[rows, par, pair(hh, g), nk * j:nk * j + nk],
                             c.qst[rows, par, pair(hh, g), S * j:S * j + S], start=g == 0, stop=False, skip_group_check=True)
                if pair_mask:
                    t.matmul(bank[0:nk, :], c.eye_bf[:], c.mask_t[:].unsqueeze(1).broadcast_to([128, 4, S]),
                             start=False, stop=False, skip_group_check=True)
                if hh == 0:
                    pe.wait_ge(max_kept, step + 1)
                for g in range(4):
                    m = t.matmul(bank[0:nk, S * g:S * g + S], c.head_sel[rows, 4 * hh + g, 0:nk], c.mt[rows, j % 2, :],
                                 start=False, stop=g == 3, skip_group_check=True)
                m.then_inc(st_full, 1)

            def values(i, par, j, hh):
                step = G * i + j
                pe.wait_ge(exped, 4 * step + hh + 1)
                if hh == 0:
                    pe.wait_ge(pj_read_a, i + 1)
                bank = c.ps_po[j % 2]
                for g in range(4):
                    t.matmul(bank[32 * g:32 * g + 32, 0:S], c.vz[0:nk, par, j, g, 32 * hh:32 * hh + 32],
                             c.p[0:nk, hh, S * g:S * g + S], start=hh == 0, stop=hh == 3, skip_group_check=True)
                for g in range(4):
                    m = t.matmul(bank[32 * g:32 * g + 32, S:2 * S], c.ones_z[0:nk, hh, :],
                                 c.p[0:nk, hh, S * g:S * g + S], start=False, stop=hh == 3, skip_group_check=True)
                m.then_inc(pv_done, 1)

            def project_out(i, par):
                pe.wait_ge(out_ready, G * i + G)
                if small(i) and i + 2 >= NG:
                    pe.wait_ge(added, N_ADD * i)
                else:
                    pe.wait_ge(pj_read_v, NV * (i + 2) + NV)
                t.matmul(c.ps_pj[1][:], wo, c.ot[:, par, :], start=True, stop=True).then_inc(wo_full, 1)

            def body(i, par):
                for j in range(G):
                    if j < G - 1:
                        nxt = lambda hh, j=j: scores(i, par, j + 1, hh)
                    elif is_last(i):
                        nxt = lambda hh: None
                    else:
                        nxt = lambda hh: scores(i + 1, 1 - par, 0, hh)
                    todo = [] if is_last(i) else {0: range(0, NV), 1: range(NV, NP), 2: (), 3: ()}[j]
                    turn_max(G * i + j, j)
                    nxt(0)
                    nxt(1)
                    scores_t(i, par, j, 0)
                    nxt(2)
                    scores_t(i, par, j, 1)
                    for u in todo[:2]:
                        project(i + 1, 1 - par, u)
                    values(i, par, j, 0)
                    nxt(3)
                    scores_t(i, par, j, 2)
                    values(i, par, j, 1)
                    scores_t(i, par, j, 3)
                    for u in todo[2:]:
                        project(i + 1, 1 - par, u)
                    values(i, par, j, 2)
                    if j == 2 and not is_first(i):
                        project_out(i - 1, 1 - par)
                    values(i, par, j, 3)

            for u in range(NP):
                project(0, 0, u)
            for hh in range(4):
                scores(0, 0, 0, hh)
            for_groups(pe, body)
            project_out(NG - 1, 1)

        @block.vector
        def _(dve):
            v = nc.vector

            def take(i, par, u):
                kind, _, half = uses[u]
                width = src_of[kind][1]
                x = 0 if kind == "q" else 1
                bank = c.ps_pj[u % 2]
                dve.wait_ge(pj_full, NP * i + u + 1)
                if not (small(i) and i < 1):
                    if rotate:
                        dve.wait_ge(turned, 2 * (i - 1) + x + 1)
                    else:
                        dve.wait_ge(low[x], i)
                if rotate:
                    table = ((c.cosq, c.sinq), (c.cos, c.sin))[x][half]
                    v.tensor_tensor(c.part[:, x, half, :].rearrange("p (r n) -> p r n", n=64),
                                    bank[:].rearrange("p (r n) -> p r n", n=64),
                                    table[:].unsqueeze(1).broadcast_to([128, 8, 64]), ALU.mult).then_inc(pj_read_v, 1)
                elif x == 0:
                    v.tensor_scalar(c.whole[:, x, 0:width], bank[:, 0:width], q_bias, SCALE, ALU.add, ALU.mult).then_inc(pj_read_v, 1)
                else:
                    v.tensor_scalar(c.whole[:, x, 0:width], bank[:, 0:width], k_bias, None, ALU.add).then_inc(pj_read_v, 1)

            def maxima(step, chunks):
                for hh in chunks:
                    dve.wait_ge(nat_full, 4 * step + hh + 1)
                    if hh == 0 and not (small(step) and step < 1):
                        dve.wait_ge(max_split, 4 * step)
                    v.tensor_reduce(c.negmax[:, 4 * hh:4 * hh + 4], c.ps_nat[hh % 2][:, 0:4 * pitch].rearrange("p (g k) -> p g k", g=4)[:, :, 0:nk],
                                    AX_X, ALU.max, negate=True).then_inc(maxed, 1)

            def split_maxima(step):
                dve.wait_ge(maxed, 4 * step + 4)
                if not (small(step) and step < 1):
                    dve.wait_ge(max_turned, step)
                nm = c.nm[:].rearrange("p (r t h) -> p r t h", r=2, t=4)
                twice = lambda ap: ap.unsqueeze(1).broadcast_to([128, 2, H])
                v.tensor_copy(nm[:, :, 0, :], twice(c.negmax[:])).then_inc(max_split, 1)
                dve.wait_ge(max_split, 4 * step + 1)
                v.tensor_tensor(c.negrest[:], c.negmax[:], nm[:, 0, 0, :], ALU.subtract).then_inc(max_split, 1)
                dve.wait_ge(max_split, 4 * step + 2)
                v.tensor_copy(nm[:, :, 1, :], twice(c.negrest[:])).then_inc(max_split, 1)
                dve.wait_ge(max_split, 4 * step + 3)
                v.tensor_tensor(nm[:, :, 2, :], twice(c.negrest[:]), nm[:, :, 1, :], ALU.subtract).then_inc(max_split, 1)

            def double(i, x, which):
                width = NT if x == 0 else wk_cols
                slots = (HIGH if which == 0 else MID)[x]
                dve.wait_ge(high if which == 0 else mid, 2 * i + x + 1)
                for to in slots[1:]:
                    m = v.tensor_copy(c.parts[:, x, to, 0:width], c.parts[:, x, slots[0], 0:width])
                if which == 1:
                    m.then_inc(doubled[x], 1)

            def normalise(i, par, j):
                step = G * i + j
                bank = c.ps_po[j % 2]
                if not (small(step) and step < 1):
                    dve.wait_ge(out_ready, step)
                dve.wait_ge(pv_done, 4 * step + 4)
                v.reciprocal(c.rden[:], bank[:, S:2 * S]).then_inc(inverted, 1)
                dve.wait_ge(inverted, step + 1)
                if j == 0 and not (small(i) and i < 2):
                    dve.wait_ge(wo_full, i - 1)
                v.tensor_tensor(c.ot[:, par, S * j:S * j + S], bank[:, 0:S], c.rden[:], ALU.mult).then_inc(out_ready, 1)

            def add_out(i):
                dve.wait_ge(wo_full, i + 1)
                if gate is None:
                    xs = c.xt[:, bass.ds(NT * i, NT)]
                    v.scalar_tensor_tensor(out=xs, in0=c.ps_pj[1][:], scalar=out_bias, in1=xs, op0=ALU.add, op1=ALU.add).then_inc(added, 1)
                else:
                    for b in range(G):
                        xs = c.xt[:, bass.ds(NT * i + S * b, S)]
                        v.scalar_tensor_tensor(out=xs, in0=c.ps_pj[1][:, S * b:S * b + S], scalar=c.mod[:, gate, bass.ds(G * i + b, 1)],
                                               in1=xs, op0=ALU.mult, op1=ALU.add).then_inc(added, 1)

            def body(i, par):
                for j in range(G):
                    nxt = not (is_last(i) and j == G - 1)
                    if nxt:
                        maxima(G * i + j + 1, (0, 1))
                    if j == 1 and not is_last(i):
                        double(i + 1, 0, 1)
                    if j > 0:
                        normalise(i, par, j - 1)
                    elif not is_first(i):
                        normalise(i - 1, 1 - par, G - 1)
                    if nxt:
                        maxima(G * i + j + 1, (2,))
                    if not is_last(i):
                        if j == 0:
                            for u in range(2):
                                take(i + 1, 1 - par, u)
                    if nxt:
                        maxima(G * i + j + 1, (3,))
                        split_maxima(G * i + j + 1)
                    if not is_last(i):
                        if j == 0:
                            for u in range(2, NV):
                                take(i + 1, 1 - par, u)
                            double(i + 1, 0, 0)
                        if j == 1:
                            double(i + 1, 1, 0)
                            double(i + 1, 1, 1)
                    if j == 2 and not is_first(i):
                        add_out(i - 1)
                    if key_mask and j == 1 and not is_last(i):
                        v.tensor_copy(c.bias_now[0:nk, 1 - par, :], c.key_bias[0:nk, bass.ds(G * (i + 1), G)]).then_inc(biased, 1)

            if key_mask:
                v.tensor_copy(c.bias_now[0:nk, 0, :], c.key_bias[0:nk, 0:G]).then_inc(biased, 1)
            for u in range(NV):
                take(0, 0, u)
            for x in range(2):
                for which in range(2):
                    double(0, x, which)
            maxima(0, range(4))
            split_maxima(0)
            for_groups(dve, body)
            normalise(NG - 1, 1, G - 1)
            add_out(NG - 1)

        @block.scalar
        def _(act):
            a = nc.scalar

            def split_high(i, par, x):
                width = NT if x == 0 else wk_cols
                act.wait_ge(turned if rotate else pj_read_v, 2 * i + x + 1)
                if not (small(i) and i < 1):
                    act.wait_ge(stacked[1 - par], 256 * pair_no(i - 1, 1 - par) + 128 * x + 128)
                a.activation(c.parts[:, x, HIGH[x][0], 0:width], c.whole[:, x, 0:width], ACT.Copy).then_inc(high, 1)

            def split_mid(i, x):
                width = NT if x == 0 else wk_cols
                act.wait_ge(rest, 2 * i + x + 1)
                a.activation(c.parts[:, x, MID[x][0], 0:width], c.whole[:, x, 0:width], ACT.Copy).then_inc(mid, 1)

            def take_values(i, par):
                act.wait_ge(pj_full, NP * i + NP)
                if not (small(i) and i < 2):
                    act.wait_ge(pv_done, 16 * (i - 1))
                for hh in range(4):
                    src = c.ps_pj[NV % 2][0:nk, :].rearrange("p (b t f) -> p b t f", b=G, t=H // 2)
                    m = a.activation(c.vz[0:nk, par, :, :, 40 * hh:40 * hh + HD],
                                     src[:, :, pair(hh, 0):pair(hh, 0) + 4, HD * (hh % 2):HD * (hh % 2) + HD], ACT.Copy)
                m.then_inc(pj_read_a, 1)

            def keep_max(step, j):
                act.wait_ge(max_turned, step + 1)
                if not (small(step) and step < 2):
                    act.wait_ge(st_full, 4 * (step - 1))
                a.activation(c.mt[:, j % 2, :], c.turned_max[j % 2], ACT.Copy).then_inc(max_kept, 1)

            def exponentials(i, par, j, hh):
                step = G * i + j
                act.wait_ge(st_full, 4 * step + hh + 1)
                if not (small(step) and step < 1):
                    act.wait_ge(pv_done, 4 * (step - 1) + hh + 1)
                if key_mask and j == 0 and hh == 0:
                    act.wait_ge(biased, i + 1)
                bias = c.bias_now[0:nk, par, j:j + 1] if key_mask else 0.0
                a.activation(c.p[0:nk, hh, :], c.ps_st[hh % 2][0:nk, :], ACT.Exp, bias=bias).then_inc(exped, 1)

            def body(i, par):
                for j in range(G):
                    keep_max(G * i + j, j)
                    exponentials(i, par, j, 0)
                    exponentials(i, par, j, 1)
                    if not is_last(i):
                        if j == 0:
                            split_high(i + 1, 1 - par, 0)
                        if j == 1:
                            split_high(i + 1, 1 - par, 1)
                        if j == 2:
                            take_values(i + 1, 1 - par)
                    exponentials(i, par, j, 2)
                    if j < 2 and not is_last(i):
                        split_mid(i + 1, j)
                    exponentials(i, par, j, 3)

            for x in range(2):
                split_high(0, 0, x)
                split_mid(0, x)
            take_values(0, 0)
            for_groups(act, body)

        @block.gpsimd
        def _(pool):
            def body(i, par):
                if not (small(i) and i < 1):
                    pool.wait_ge(pj_full, NP * i)
                nc.gpsimd.tensor_copy(c.kv_now[:, 0:wk_cols], kv_src[:, bass.ds(wk_cols * i, wk_cols)]).then_inc(kv_here, 1)
                for x in range(2):
                    w = slice(0, NT if x == 0 else wk_cols)
                    if rotate:
                        pool.wait_ge(pj_read_v, NV * i + 2 * x + 2)
                        if not (small(i) and i < 1):
                            pool.wait_ge(low[x], i)
                        nc.gpsimd.tensor_tensor(c.whole[:, x, :], c.part[:, x, 0, :], c.part[:, x, 1, :], ALU.add).then_inc(turned, 1)
                    pool.wait_ge(high, 2 * i + x + 1)
                    nc.gpsimd.tensor_tensor(c.whole[:, x, w], c.whole[:, x, w], c.parts[:, x, HIGH[x][0], w], ALU.subtract).then_inc(rest, 1)
                    pool.wait_ge(mid, 2 * i + x + 1)
                    nc.gpsimd.tensor_tensor(c.parts[:, x, LOW[x], w], c.whole[:, x, w], c.parts[:, x, MID[x][0], w], ALU.subtract).then_inc(low[x], 1)
            for_groups(pool, body)

        @block.sync
        def _(sp):
            def body(i, par):
                number = (lambda v: v) if small(i) else sp.snap
                done = number(i + 1)
                for x in range(2):
                    width = NT if x == 0 else wk_cols
                    st = c.qst if x == 0 else c.kst
                    sp.wait_ge(doubled[x], done)
                    sp.wait_ge(low[x], done)
                    for t in range(H // 2):
                        sp.dma_start(st[:, par, t, 0:width], c.parts[16 * t:16 * t + 16, x, :, 0:width]).then_inc(stacked[par], 16)
            for_groups(sp, body)


def pair_no(i, par):
    if isinstance(i, int):
        return i // 2
    return (i - par) // 2


def mlp_phase(nc, c, ctx):
    s = lambda x: ctx.enter_context(nc.semaphore("mlp" + x))
    up_full, gelued, down_full, gated, added = s("_up_full"), s("_gelued"), s("_down_full"), s("_gated"), s("_added")
    NF = F // 128
    with nc.Block() as block:
        @block.tensor
        def _(pe):
            banks = [c.ps_nat[0], c.ps_nat[1], c.ps_st[0], c.ps_st[1]]

            def up(i, f):
                if not (isinstance(i, int) and i < 1):
                    pe.wait_ge(gelued, NF * (i - 1) + f + 1)
                nc.tensor.matmul(banks[f][:], c.w1[:, 128 * f:128 * f + 128], c.ht[:, bass.ds(NT * i, NT)], start=True, stop=True).then_inc(up_full, 1)

            def body(i, par):
                if not (isinstance(i, int) and i < 2):
                    pe.wait_ge(gated, G * (i - 1))
                for f in range(NF):
                    if not is_last(i):
                        up(i + 1, f)
                    pe.wait_ge(gelued, NF * i + f + 1)
                    m = nc.tensor.matmul(c.ps_pj[par][:], c.w2[:, f, :], c.hid[par][f], start=f == 0, stop=f == NF - 1)
                m.then_inc(down_full, 1)
            for f in range(NF):
                up(0, f)
            for_groups(pe, body)

        @block.scalar
        def _(act):
            banks = [c.ps_nat[0], c.ps_nat[1], c.ps_st[0], c.ps_st[1]]

            def body(i, par):
                if not (isinstance(i, int) and i < 2):
                    act.wait_ge(down_full, i - 1)
                for f in range(NF):
                    act.wait_ge(up_full, NF * i + f + 1)
                    nc.scalar.activation(c.hid[par][f], banks[f][:], ACT.Gelu_apprx_tanh, bias=c.vec[:, c.vec_row["L0_xcond_mlp_b1"] + f:c.vec_row["L0_xcond_mlp_b1"] + f + 1]).then_inc(gelued, 1)
            for_groups(act, body)

        @block.vector
        def _(dve):
            def body(i, par):
                dve.wait_ge(down_full, i + 1)
                if not (isinstance(i, int) and i < 2):
                    dve.wait_ge(added, i - 1)
                for b in range(G):
                    nc.vector.tensor_scalar(c.xn[:, par, S * b:S * b + S], c.ps_pj[par][:, S * b:S * b + S], c.vec[:, c.vec_row["L0_xcond_mlp_b2"]:c.vec_row["L0_xcond_mlp_b2"] + 1],
                                            c.mod[:, 8, bass.ds(G * i + b, 1)], ALU.add, ALU.mult).then_inc(gated, 1)
            for_groups(dve, body)

        @block.gpsimd
        def _(pool):
            def body(i, par):
                pool.wait_ge(gated, G * (i + 1))
                xs = c.xt[:, bass.ds(NT * i, NT)]
                nc.gpsimd.tensor_tensor(xs, xs, c.xn[:, par, :], ALU.add).then_inc(added, 1)
            for_groups(pool, body)


def store_phase(nc, c, out, ctx):
    s = lambda x: ctx.enter_context(nc.semaphore("out" + x))
    fetched, turned, copied = s("_fetched"), s("_turned"), s("_copied")
    stored = [s("_stored0"), s("_stored1")]
    with nc.Block() as block:
        @block.scalar
        def _(act):
            def body(i, par):
                if not (isinstance(i, int) and i < 2):
                    act.wait_ge(turned, i - 1)
                nc.scalar.activation(c.ot[:, par, :], c.xt[:, bass.ds(NT * i, NT)], ACT.Copy).then_inc(fetched, 1)
            for_groups(act, body)

        @block.tensor
        def _(pe):
            def body(i, par):
                pe.wait_ge(fetched, i + 1)
                if not (isinstance(i, int) and i < 2):
                    pe.wait_ge(copied, i - 1)
                for b in range(G):
                    m = nc.tensor.transpose(c.ps_st[par][:, S * b:S * b + S], c.ot[:, par, S * b:S * b + S], c.eye[:])
                m.then_inc(turned, 1)
            for_groups(pe, body)

        @block.vector
        def _(dve):
            def body(i, par):
                dve.wait_ge(turned, i + 1)
                if not (isinstance(i, int) and i < 2):
                    dve.wait_ge(stored[par], 16 * pair_no(i, par))
                nc.vector.tensor_copy(c.in_x[:, par].rearrange("p b d -> p (b d)"), c.ps_st[par][:]).then_inc(copied, 1)
            for_groups(dve, body)

        @block.sync
        def _(sp):
            def body(i, par):
                sp.wait_ge(copied, i + 1)
                sp.dma_start(out[bass.ds(G * i, G)].rearrange("b s d -> s b d"), c.in_x[:, par]).then_inc(stored[par], 16)
            for_groups(sp, body)
            sp.wait_ge(stored[0], 16 * NG // 2)
            sp.wait_ge(stored[1], 16 * NG // 2)


def two_layers(nc, ins, out):
    with ExitStack() as ctx:
        c = Core()

        def sb(name, shape, dt=F32):
            return ctx.enter_context(nc.sbuf_tensor(name, shape, dt))

        c.xt = sb("xt", [D, B * S])
        c.ht = sb("ht", [D, B * S])
        c.ct = sb("ct", [D, B * SC])
        c.wqkv = sb("wqkv", [D, 3 * D])
        c.wrot = sb("wrot", [D, 2, D])
        c.w0 = sb("w0", [D, 5, D])
        c.w1 = sb("w1", [D, F])
        c.w2 = sb("w2", [128, F // 128, D])
        c.wq = sb("wq", [D, D])
        c.wkv = sb("wkv", [D, 2 * D])
        c.wp = sb("wp", [D, D])
        c.vec = sb("vec", [128, NVEC])
        c.bp = sb("bp", [128, 1])
        c.cos = sb("cos", [128, 64])
        c.sin = sb("sin", [128, 64])
        c.cosq = sb("cosq", [128, 64])
        c.sinq = sb("sinq", [128, 64])
        c.mask8 = sb("mask8", [S, S], U8)
        c.key8 = sb("key8", [128, SC], U8)
        c.mask_nat = sb("mask_nat", [S, S], BF16)
        c.mask_t = sb("mask_t", [S, S], BF16)
        c.key_bias = sb("key_bias", [128, B])
        c.bias_now = sb("bias_now", [128, 2, G])
        c.key_rows = sb("key_rows", [128, SC], BF16)
        c.eye = sb("eye", [128, 128])
        c.eye_bf = sb("eye_bf", [128, 128], BF16)
        c.pick = sb("pick", [128, H])
        c.head_sel = sb("head_sel", [128, H, S], BF16)
        c.mean = sb("mean", [D, D])
        c.centre = sb("centre", [D, D])
        c.eps = sb("eps", [128, 1])
        c.ones_z = sb("ones_z", [128, 4, 32])
        c.mod = sb("mod", [D, 13, B])
        c.part = sb("part", [D, 2, 2, NT])
        c.whole = sb("whole", [D, 2, NT])
        c.parts = sb("parts", [D, 2, SLOTS, NT], BF16)
        c.qst = sb("qst", [128, 2, H // 2, NT], BF16)
        c.kst = sb("kst", [128, 2, H // 2, NT], BF16)
        c.vz = sb("vz", [128, 2, G, 4, 160])
        c.p = sb("p", [128, 4, NT])
        c.kv_now = sb("kv_now", [D, NT])
        c.negmax = sb("negmax", [S, H])
        c.nm = sb("nm", [S, 128], BF16)
        c.negrest = sb("negrest", [S, H])
        c.mt = sb("mt", [128, 2, S], BF16)
        c.rden = sb("rden", [D, S])
        c.ot = sb("ot", [D, 2, NT])
        c.hid = [[c.part[:, 0, 0], c.part[:, 0, 1], c.part[:, 1, 0], c.part[:, 1, 1]],
                 [c.whole[:, 0], c.whole[:, 1], c.p[:, 2], c.p[:, 3]]]
        c.sq, c.sd, c.rs, c.xn = c.part[:, 0], c.part[:, 1], c.whole[:], c.p[:, 0:2]
        c.in_x = c.p[:, 0:2].rearrange("p a (b d) -> p a b d", d=D)
        c.in_c = c.p[:, 2:4].rearrange("p a (b d) -> p a b d", d=D)
        c.ada_w = c.ht[:, 0:9 * D]
        c.wss = c.ht[:, 9 * D:13 * D].rearrange("p (a n) -> p a n", a=2)
        c.wp_in = c.ht[:, 16 * D:17 * D]
        c.cond = c.ht[0:B, 17 * D:18 * D]
        c.cond_t = c.ht[:, 18 * D:19 * D].rearrange("p (a b) -> p a b", a=2)
        c.vec_rows = c.ht[0:NVEC, 19 * D:20 * D]
        ps = lambda name, dt=F32: ctx.enter_context(nc.psum_tensor(name, [128, 512], dt))
        c.vec_row = VEC_ROW
        c.ps_nat = [ps("ps_nat0"), ps("ps_nat1")]
        c.ps_st = [ps("ps_st0"), ps("ps_st1")]
        c.ps_pj = [ps("ps_pj0"), ps("ps_pj1")]
        c.ps_po = [ps("ps_po0"), ps("ps_po1")]
        c.turned_max = [bank[:, 2 * S:2 * S + S // 2].bitcast(BF16) for bank in c.ps_po]
        c.turned_mask = c.ps_po[0][:].bitcast(BF16)

        setup_phase(nc, c, ins, ctx)
        load_phase(nc, c, ins["x"], ins["ctx_1024"], ctx)
        norm_phase(nc, c, "n1", c.xt, c.ht, S, 1, 0, ctx)
        attention_phase(nc, c, "sa", ctx, nk=S, kv_src=c.ht, wq=c.wqkv[:, 0:D], wk=c.wqkv[:, D:2 * D], wv=c.wqkv[:, 2 * D:3 * D],
                        wo=c.w0[:, 0, :], rotate=True, pair_mask=True, gate=2)
        norm_phase(nc, c, "n2", c.xt, c.ht, S, 4, 3, ctx)
        attention_phase(nc, c, "ca", ctx, nk=SC, kv_src=c.ct, wq=c.w0[:, 1, :], wk=c.w0[:, 2, :], wv=c.w0[:, 3, :], wo=c.w0[:, 4, :],
                        q_bias=0.0, k_bias=0.0, key_mask=True, gate=5)
        norm_phase(nc, c, "n3", c.xt, c.ht, S, 7, 6, ctx)
        mlp_phase(nc, c, ctx)
        norm_phase(nc, c, "n4", c.xt, c.ht, S, 9, 10, ctx)
        norm_phase(nc, c, "n5", c.ct, c.ct, SC, 11, 12, ctx)
        attention_phase(nc, c, "xa", ctx, nk=SC, kv_src=c.ct, wq=c.wq[:], wk=c.wkv[:, 0:D], wv=c.wkv[:, D:2 * D], wo=c.wp[:],
                        q_bias=c.vec[:, VEC_ROW["L1_xcond_bq"]:VEC_ROW["L1_xcond_bq"] + 1],
                        k_bias=c.vec[:, VEC_ROW["L1_xcond_bkv"]:VEC_ROW["L1_xcond_bkv"] + 1], out_bias=c.bp[:, 0:1])
        store_phase(nc, c, out, ctx)


def rope_tables():
    n = 64
    inv = 1.0 / 10000.0 ** (np.arange(0, HD, 2, dtype=np.float32) / HD)
    freqs = np.outer(np.arange(n, dtype=np.float32), inv)
    emb = np.concatenate([freqs, freqs], axis=-1)
    cos, sin = np.cos(emb).astype(np.float32), np.sin(emb).astype(np.float32)
    sin[:, :HD // 2] *= -1
    return np.ascontiguousarray(np.tile(cos.T, (H, 1))), np.ascontiguousarray(np.tile(sin.T, (H, 1)))


_INS = ["x", "cond_1024", "ctx_1024", "mask_BxS2_bf1", "mask_SxS_bk0"] + ["L0_xcond_" + n for n in (
    "adaLN_W", "adaLN_b", "norm1_w", "qkv_W", "attn_out_W", "normc_w", "cq_W", "ck_W", "cv_W", "co_W", "norm2_w",
    "mlp_W1", "mlp_b1", "mlp_W2", "mlp_b2")] + ["L1_xcond_" + n for n in (
        "Wq", "bq", "Wkv", "bkv", "Wp", "bp", "Wss_q", "bss_q", "Wss_kv", "bss_kv")]


def kernel(**inputs):
    import concourse.bacc as _bacc
    from concourse.bass_utils import run_bass_kernel_spmd as _run

    nc = _bacc.Bacc("TRN2", target_bir_lowering=False, num_devices=1)
    cos, sin = rope_tables()
    arrays, args = {}, {}

    def give(name, a):
        a = np.ascontiguousarray(a)
        if a.dtype == np.bool_:
            a = a.view(np.uint8 if a.shape[-1] % 4 else np.int32)
        arrays[f"in_{name}_dram"] = a
        args[name] = nc.dram_tensor(f"in_{name}_dram", a.shape, mybir.dt.from_np(a.dtype), kind="ExternalInput").ap()

    for name in _INS:
        give(name, inputs[name])
    give("cos", cos)
    give("sin", sin)
    out = nc.dram_tensor("out_0_dram", (B, S, D), F32, kind="ExternalOutput").ap()
    two_layers(nc, args, out)
    r = _run(nc, [arrays], core_ids=[0])
    return r.results[0]["out_0_dram"]
```
